# Optimizing a Trainium2 kernel written in Bass

```python
import numpy as np
import jax
import jax.numpy as jnp

def _softmax(x, axis=-1):
    return jax.nn.softmax(x, axis=axis)

def _gelu(x):
    return jax.nn.gelu(x, approximate=True)

def _silu(x):
    return jax.nn.silu(x)

def _sigmoid(x):
    return jax.nn.sigmoid(x)

def _layernorm(x, axis=-1, eps=1e-05):
    m = jnp.mean(x, axis=axis, keepdims=True)
    v = jnp.var(x, axis=axis, keepdims=True)
    return (x - m) / jnp.sqrt(v + eps)

def _scatter_add(tgt, idx, src, axis=0):
    return tgt.at[idx].add(src)

def _segment_sum(src, seg, n):
    return jax.ops.segment_sum(src, seg, n)
kernel_name = 'mk_adj_preln_d4_adj_r2_cc2d4e'

def setup_inputs(seed: int=0):
    np.random.seed(seed)
    _w = jnp.asarray

    def _rec_inputs():
        import jax
        import jax.numpy as jnp
        _gk = jax.random.key(seed)
        x = 7.22e-05 + 1 * jax.random.normal(jax.random.fold_in(_gk, 1), (8, 1024, 128), jnp.float32)
        _w = (1.0 + jnp.arange(1024, dtype=jnp.float32)) ** (-0.5)
        _w = _w / _w.mean()
        _pij = jnp.clip(0.00390625 * _w[:, None] * _w[None, :], 0.0, 1.0)
        _a = jax.random.uniform(jax.random.fold_in(_gk, 2), (8, 1024, 1024)) < _pij
        _a = jnp.logical_or(_a, jnp.eye(1024, dtype=bool))
        _af = _a.astype(jnp.float32)
        _af = _af * jax.random.uniform(jax.random.fold_in(_gk, 3), (8, 1024, 1024), jnp.float32, 0.05, 1)
        adj = _af
        return (x, adj)
    x, adj = _rec_inputs()

    def _L0_gnn_setup():
        import jax, jax.numpy as jnp
        import numpy as np
        D_IN = 128
        D_HID = 256
        key = jax.random.key(seed)
        k1, k2, k3, k4, k5, k6 = jax.random.split(key, 6)
        x = jax.random.normal(k1, (8, 2048, D_IN), dtype=jnp.float32)
        adj = jax.random.uniform(k2, (8, 2048, 2048), dtype=jnp.float32)
        s1 = 1.0 / np.sqrt(D_IN)
        s2 = 1.0 / np.sqrt(D_HID)
        W1 = jax.random.uniform(k3, (D_IN, D_HID), dtype=jnp.float32, minval=-s1, maxval=s1)
        b1 = jax.random.uniform(k4, (D_HID,), dtype=jnp.float32, minval=-s1, maxval=s1)
        W2 = jax.random.uniform(k5, (D_HID, D_IN), dtype=jnp.float32, minval=-s2, maxval=s2)
        b2 = jax.random.uniform(k6, (D_IN,), dtype=jnp.float32, minval=-s2, maxval=s2)
        eps = jnp.zeros((1,), dtype=jnp.float32)
        return {'x': x, 'adj': adj, 'eps': eps, 'W1': W1, 'b1': b1, 'W2': W2, 'b2': b2}
    _L0_gnn_all = _L0_gnn_setup()
    _L0_gnn_in = {k: v for k, v in _L0_gnn_all.items() if k in ('eps', 'W1', 'b1', 'W2', 'b2')}
    del _L0_gnn_all

    def _L1_gnn_setup():
        import jax, jax.numpy as jnp
        import numpy as np
        B, N, DIN, DOUT = (16, 512, 128, 128)
        key = jax.random.key(seed)
        k1, k2, k3, k4 = jax.random.split(key, 4)
        x = jax.random.normal(k1, (B, N, DIN), dtype=jnp.float32)
        adj = jax.random.uniform(k2, (B, N, N), dtype=jnp.float32)
        W = jax.random.normal(k3, (DOUT, DIN), dtype=jnp.float32) * (1.0 / np.sqrt(DIN))
        b = jax.random.normal(k4, (DOUT,), dtype=jnp.float32) * 0.01
        return {'x': x, 'adj': adj, 'W': W, 'b': b}
    _L1_gnn_all = _L1_gnn_setup()
    _L1_gnn_in = {k: v for k, v in _L1_gnn_all.items() if k in ('W', 'b')}
    del _L1_gnn_all

    def _L2_gnn_setup():
        import math
        import jax, jax.numpy as jnp
        import numpy as np
        B, N, D, H = (32, 256, 128, 8)
        HD = D // H
        key = jax.random.key(seed)
        ks = jax.random.split(key, 9)
        h = jax.random.normal(ks[0], (B, N, D), dtype=jnp.float32)
        edge = jax.random.normal(ks[1], (B, N, N), dtype=jnp.float32)
        adj = jax.random.uniform(ks[2], (B, N, N)) < 0.5
        adj_mask = adj | jnp.eye(N, dtype=bool)[None]
        s = 1.0 / math.sqrt(D)
        W_q = jax.random.normal(ks[3], (D, D), dtype=jnp.float32) * s
        W_k = jax.random.normal(ks[4], (D, D), dtype=jnp.float32) * s
        W_v = jax.random.normal(ks[5], (D, D), dtype=jnp.float32) * s
        W_e = jax.random.normal(ks[6], (H, 1), dtype=jnp.float32)
        W_o = jax.random.normal(ks[7], (D, D), dtype=jnp.float32) * s
        return {'h': h, 'edge': edge, 'adj_mask': adj_mask, 'W_q': W_q, 'W_k': W_k, 'W_v': W_v, 'W_e': W_e, 'W_o': W_o}
    _L2_gnn_all = _L2_gnn_setup()
    _L2_gnn_in = {k: v for k, v in _L2_gnn_all.items() if k in ('W_q', 'W_k', 'W_v', 'W_e', 'W_o')}
    del _L2_gnn_all

    def _L3_gnn_setup():
        import jax, jax.numpy as jnp
        import numpy as np
        B, N, F = (2, 1024, 128)
        OUT = 128
        H = 4
        NEG_SLOPE = 0.2
        key = jax.random.key(seed)
        ks = jax.random.split(key, 10)
        inputs = jax.random.normal(ks[0], (B, N, F), dtype=jnp.float32)
        adj = jax.random.bernoulli(ks[1], 0.02, (B, N, N)).astype(jnp.float32)
        adj = jnp.maximum(adj, jnp.eye(N, dtype=jnp.float32)[None])
        adj_seq = jax.random.normal(ks[2], (B, N, N), dtype=jnp.float32)
        s = 1.0 / np.sqrt(F)
        W = jax.random.normal(ks[3], (H, F, OUT), dtype=jnp.float32) * s
        so = 1.0 / np.sqrt(OUT)
        w1 = jax.random.normal(ks[4], (H, OUT), dtype=jnp.float32) * so
        b1 = jnp.zeros((H,), dtype=jnp.float32)
        w2 = jax.random.normal(ks[5], (H, OUT), dtype=jnp.float32) * so
        b2 = jnp.zeros((H,), dtype=jnp.float32)
        alpha = jnp.full((H,), 0.5, dtype=jnp.float32)
        bias = jnp.zeros((H, OUT), dtype=jnp.float32)
        return {'inputs': inputs, 'adj': adj, 'adj_seq': adj_seq, 'W': W, 'w1': w1, 'b1': b1, 'w2': w2, 'b2': b2, 'alpha': alpha, 'bias': bias}
    _L3_gnn_all = _L3_gnn_setup()
    _L3_gnn_in = {k: v for k, v in _L3_gnn_all.items() if k in ('W', 'w1', 'b1', 'w2', 'b2', 'alpha', 'bias')}
    del _L3_gnn_all
    return {'x': x, 'adj': adj, 'L0_gnn_eps': _L0_gnn_in['eps'], 'L0_gnn_W1': _L0_gnn_in['W1'], 'L0_gnn_b1': _L0_gnn_in['b1'], 'L0_gnn_W2': _L0_gnn_in['W2'], 'L0_gnn_b2': _L0_gnn_in['b2'], 'L1_gnn_W': _L1_gnn_in['W'], 'L1_gnn_b': _L1_gnn_in['b'], 'L2_gnn_W_q': _L2_gnn_in['W_q'], 'L2_gnn_W_k': _L2_gnn_in['W_k'], 'L2_gnn_W_v': _L2_gnn_in['W_v'], 'L2_gnn_W_e': _L2_gnn_in['W_e'], 'L2_gnn_W_o': _L2_gnn_in['W_o'], 'L3_gnn_W': _L3_gnn_in['W'], 'L3_gnn_w1': _L3_gnn_in['w1'], 'L3_gnn_b1': _L3_gnn_in['b1'], 'L3_gnn_w2': _L3_gnn_in['w2'], 'L3_gnn_b2': _L3_gnn_in['b2'], 'L3_gnn_alpha': _L3_gnn_in['alpha'], 'L3_gnn_bias': _L3_gnn_in['bias']}

def reference(x, adj, L0_gnn_eps, L0_gnn_W1, L0_gnn_b1, L0_gnn_W2, L0_gnn_b2, L1_gnn_W, L1_gnn_b, L2_gnn_W_q, L2_gnn_W_k, L2_gnn_W_v, L2_gnn_W_e, L2_gnn_W_o, L3_gnn_W, L3_gnn_w1, L3_gnn_b1, L3_gnn_w2, L3_gnn_b2, L3_gnn_alpha, L3_gnn_bias):
    import jax
    import jax.numpy as jnp

    def _L0_gnn_ref(x, adj, eps, W1, b1, W2, b2):
        import jax, jax.numpy as jnp
        import numpy as np
        D_IN = 128
        D_HID = 256
        aggregated = jnp.einsum('bnm,bmd->bnd', adj, x)
        h = (1.0 + eps) * x + aggregated
        h = jax.nn.relu(h @ W1 + b1)
        return h @ W2 + b2

    def _L1_gnn_ref(x, adj, W, b):
        import jax, jax.numpy as jnp
        import numpy as np
        B, N, DIN, DOUT = (16, 512, 128, 128)
        n = adj.shape[-1]
        adj_hat = adj + jnp.eye(n, dtype=adj.dtype)
        deg = jnp.sum(adj_hat, axis=-1)
        d_inv_sqrt = jnp.where(deg > 0, deg ** (-0.5), 0.0)
        norm_adj = d_inv_sqrt[:, :, None] * adj_hat * d_inv_sqrt[:, None, :]
        agg = jnp.einsum('bnm,bmf->bnf', norm_adj, x)
        out = jnp.einsum('bnf,of->bno', agg, W) + b
        return jax.nn.relu(out)

    def _L2_gnn_ref(h, edge, adj_mask, W_q, W_k, W_v, W_e, W_o):
        import math
        import jax, jax.numpy as jnp
        import numpy as np
        B, N, D, H = (32, 256, 128, 8)
        HD = D // H
        b, n, _ = h.shape
        q = (h @ W_q.T).reshape(b, n, H, HD).transpose(0, 2, 1, 3)
        k = (h @ W_k.T).reshape(b, n, H, HD).transpose(0, 2, 1, 3)
        v = (h @ W_v.T).reshape(b, n, H, HD).transpose(0, 2, 1, 3)
        edge_bias = jnp.einsum('bij,h->bhij', edge, W_e[:, 0])
        scores = jnp.einsum('bhid,bhjd->bhij', q, k) / math.sqrt(HD) + edge_bias
        scores = jnp.where(adj_mask[:, None], scores, -jnp.inf)
        attn = jax.nn.softmax(scores, axis=-1)
        out = jnp.einsum('bhij,bhjd->bhid', attn, v)
        out = out.transpose(0, 2, 1, 3).reshape(b, n, D)
        return out @ W_o.T

    def _L3_gnn_ref(inputs, adj, adj_seq, W, w1, b1, w2, b2, alpha, bias):
        import jax, jax.numpy as jnp
        import numpy as np
        B, N, F = (2, 1024, 128)
        OUT = 128
        H = 4
        NEG_SLOPE = 0.2
        bias_mat = -1000000000.0 * (1.0 - adj)
        coefs_adj = jax.nn.softmax(adj_seq, axis=-1)

        def head(Wh, w1h, b1h, w2h, b2h, ah, bh):
            fts = jnp.einsum('bnf,fo->bno', inputs, Wh)
            f1 = fts @ w1h + b1h
            f2 = fts @ w2h + b2h
            logits = f1[:, :, None] + f2[:, None, :]
            coefs_logits = jax.nn.softmax(jax.nn.leaky_relu(logits, NEG_SLOPE) + bias_mat, axis=-1)
            coefs = ah * coefs_logits + (1.0 - ah) * coefs_adj
            vals = jnp.einsum('bnm,bmo->bno', coefs, fts) + bh
            return jax.nn.elu(vals + inputs)
        outs = jax.vmap(head)(W, w1, b1, w2, b2, alpha, bias)
        return jnp.mean(outs, axis=0)
    h = jnp.maximum(_layernorm(x, axis=-1), 0.0)
    x = x + _L0_gnn_ref(h, adj, L0_gnn_eps, L0_gnn_W1, L0_gnn_b1, L0_gnn_W2, L0_gnn_b2)
    h = jnp.maximum(_layernorm(x, axis=-1), 0.0)
    x = x + _L1_gnn_ref(h, adj, L1_gnn_W, L1_gnn_b)
    h = jnp.maximum(_layernorm(x, axis=-1), 0.0)
    x = x + _L2_gnn_ref(h, adj, adj, L2_gnn_W_q, L2_gnn_W_k, L2_gnn_W_v, L2_gnn_W_e, L2_gnn_W_o)
    h = jnp.maximum(_layernorm(x, axis=-1), 0.0)
    x = x + _L3_gnn_ref(h, adj, adj, L3_gnn_W, L3_gnn_w1, L3_gnn_b1, L3_gnn_w2, L3_gnn_b2, L3_gnn_alpha, L3_gnn_bias)
    return x

_drawn_inputs = setup_inputs


def setup_inputs(seed=0):
    import zlib

    import numpy as np

    out = dict(_drawn_inputs(seed))
    spreads = {'L3_gnn_b1': (0.0, 0.1),
     'L3_gnn_b2': (0.0, 0.1),
     'L3_gnn_alpha': (0.5, 0.6),
     'L3_gnn_bias': (0.0, 0.327)}
    factors = {'L0_gnn_b1': 3.434, 'L1_gnn_b': 7.975}
    for name, (base, spread) in spreads.items():
        noise = np.random.default_rng([zlib.crc32(name.encode()), seed]).standard_normal(out[name].shape)
        drawn = base * np.exp(spread * noise) if base else spread * noise
        out[name] = jnp.asarray(drawn.astype(out[name].dtype))
    for name, factor in factors.items():
        out[name] = (out[name] * factor).astype(out[name].dtype)
    return out
```

```python
from contextlib import ExitStack

import numpy as np

import concourse.bass as bass
from concourse import mybir

F32 = mybir.dt.float32
BF16 = mybir.dt.bfloat16
I32 = mybir.dt.int32
ALU = mybir.AluOpType
ACT = mybir.ActivationFunctionType
AX = mybir.AxisListType

P = 128
MASKED = -1.0e30
PENALTY = 1.0e9
LN_EPS = 1e-5
TINY = 1e-20
LEAK = 0.2


def graph_layers(nc, x_in, adj, eps0, W1, b1, W2, b2, Wg, bg, Wq, Wk, Wv, We, Wo,
                 W3, w31, b31, w32, b32, alpha, bias3, out, scratch, shifts):
    NB, N, D = x_in.shape
    T = N // P
    C1 = W1.shape[1] // P
    H = We.shape[0]
    HD = D // H
    H3 = W3.shape[0]
    HALF = 512
    NH = N // HALF
    PARTS = 3
    KS = 6 * HD
    RING = 8
    AR = 4
    SCALE = float(HD) ** -0.5
    OWN = 60
    assert D == P and C1 * P == W1.shape[1] and NH == 2 and (T * H + T + T * H3) % RING == 0

    uses, count = {}, [0] * 4

    def use(unit, *key):
        uses[key] = (unit, count[unit])
        count[unit] += 1

    for t in range(T):
        use(t % 4, "adjT", t)
    use(0, "agg", 0)
    for c in range(C1):
        use(1 + c, "hid", c)
    use(3, "mlp")
    use(0, "agg", 1)
    use(1, "lin1")
    use(2, "hT", 2)
    use(3, "q")
    use(0, "k")
    use(1, "v")
    for h in range(H):
        for t in range(T):
            use((h * T + t) % 4, "max", h, t)
    use(0, "maxT")
    use(2, "pv", 0)
    use(3, "pv", 1)
    for j in range(T):
        for h in range(H):
            use(h % 2, "score", j, h)
    for g in range(2):
        use(g, "oN", g)
    use(2, "oT")
    use(3, "wo")
    use(0, "hT", 3)
    use(1, "f2")
    use(2, "amax")
    for h in range(H3):
        use(h % 2, "f1", h)
    for t in range(T):
        use(t % 2, "fts", t)
    use(3, "ca")
    for h in range(H3):
        use(h % 2, "num", h)
        use(2, "den", h)
    use(3, "denT")
    for t in range(T):
        use(t % 2, "tail", t)

    with ExitStack() as ctx:
        def sb(name, shape, dt=F32):
            return ctx.enter_context(nc.sbuf_tensor(name, shape, dt))

        def sem(name):
            return ctx.enter_context(nc.semaphore(name))

        U = [ctx.enter_context(nc.psum_tensor(f"U{i}", [P, N], F32)) for i in range(4)]

        ident = sb("ident", [P, P])
        identE = sb("identE", [P, P])
        w1 = sb("w1", [P, C1 * P])
        w2 = sb("w2", [P, C1, P])
        b1c = sb("b1c", [P, C1])
        b2r = sb("b2r", [P, P])
        bgr = sb("bgr", [P, P])
        ring = sb("ring", [P, RING, N])
        flat = ring[:, :, :].rearrange("p k n -> p (k n)")
        wnat = flat[:, 0:5 * P].rearrange("p (k d) -> p k d", k=5)
        w3v = flat[:, N:2 * N].rearrange("p (k h d) -> p k h d", k=2, h=H3)
        utmp = flat[:, 2 * N:2 * N + H3 * P].rearrange("p (h d) -> p h d", h=H3)
        wT = sb("wT", [P, 5, P])
        w3 = sb("w3", [P, H3, P])
        b3r = sb("b3r", [P, H3, P])
        u12 = sb("u12", [P, 2, H3])
        u1rep = sb("u1rep", [P, H3, P])
        ones = sb("ones", [P, P])
        col = sb("col", [P, 64])
        epsc, wec, b31c, b32c, alc = col[:, 0:1], col[:, 1:1 + H], col[:, 10:10 + H3], col[:, 14:14 + H3], col[:, 18:18 + H3]
        oneE, wabs, wpos, oma, mhalf = col[:, 22:23], col[:, 24:24 + H], col[:, 32:32 + H], col[:, 40:40 + H3], col[:, 48:48 + T]
        wneg = col[:, 56:56 + H]
        signf = sb("signf", [P, H])
        signi = sb("signi", [P, H], I32)

        adjN = sb("adjN", [P, AR, N])
        adjT = sb("adjT", [P, T, N])
        pm = sb("pm", [P, 2 * 2 * N])
        hb = pm[:, :].rearrange("p (t c) -> p t c", t=T)
        m0 = sb("m0", [P, N])
        stacks = sb("stacks", [P, 2 * H * N], BF16)
        qs = stacks[:, 0:H * N].rearrange("p (h n) -> p h n", h=H)
        ks = stacks[:, H * N:].rearrange("p (h n) -> p h n", h=H)
        s32 = stacks[:, :].bitcast(F32)
        vals = s32[:, 0:T * H3 * P].rearrange("p (t h d) -> p t h d", t=T, h=H3)
        numT = s32[:, T * H3 * P:].rearrange("p (h n) -> p h n", h=H3)
        maskN = sb("maskN", [P, T, N], BF16)
        rho = maskN[:, :, :].rearrange("p t n -> p (t n)").bitcast(F32).rearrange("p (h n) -> p h n", h=H3)
        misc = sb("misc", [P, 3 * N])
        parts = misc[:, :].bitcast(BF16).rearrange("p (s k n) -> p s k n", s=2, k=PARTS)
        hid = misc[:, 0:C1 * N].rearrange("p (c n) -> p c n", c=C1)
        tail = misc[:, :].rearrange("p (k c) -> p k c", c=HALF)
        va = sb("va", [P, T, H, 32])
        denS = va[:, :, :, :].rearrange("p t h c -> p (t h c)").rearrange("p (h n) -> p h n", h=H3)
        xin = sb("xin", [P, T, P])
        x = sb("x", [P, T, P])
        hN = sb("hN", [P, T, P])
        hT = sb("hT", [P, N])
        tmpT = sb("tmpT", [P, N])
        drep = m0[:, :].rearrange("p (t h c) -> p t h c", t=T, h=H3)
        st = sb("st", [P, T, 6])
        mv = sb("mv", [P, T, 2])
        stat = sb("stat", [P, 16, T])
        amax, namax, asum, esum, ve, rstd, nm, deg, dinv, dpos, degc, re = [stat[:, i, :] for i in range(12)]
        mx = sb("mx", [P, H, T])
        mneg = sb("mneg", [P, H, T])
        mrow = sb("mrow", [H * T, P], BF16)
        rden = sb("rden", [P, T, H // 2])
        f2 = sb("f2", [P, T, H3])
        f2m = sb("f2m", [P, T, H3])
        tj = sb("tj", [P, T, H3])
        dj = sb("dj", [P, T, H3])
        sm3 = sb("sm3", [P, 4, H3])
        f2p, f2x, cb = sm3[:, 0, :], sm3[:, 1, :], sm3[:, 2, :]
        den = sb("den", [P, H3, T])
        r1 = sb("r1", [P, H3, T])
        r2 = sb("r2", [P, H3, T])

        w_in = sem("w_in")
        setup_pool = sem("setup_pool")
        setup_dve = sem("setup_dve")
        setup_pe = sem("setup_pe")
        adj_in = [sem(f"adj_in{i}") for i in range(AR)]
        adj_max = sem("adj_max")
        adj_sum = sem("adj_sum")
        x_loaded = sem("x_loaded")
        x_taken = sem("x_taken")
        x_based = sem("x_based")
        x_stored = sem("x_stored")
        x_final = sem("x_final")
        full = [sem(f"full{i}") for i in range(4)]
        free = [sem(f"free{i}") for i in range(4)]
        dve_own = sem("dve_own")
        pool_own = sem("pool_own")
        act_own = sem("act_own")
        passed = sem("passed")
        relu_neg = sem("relu_neg")
        mneg_ready = sem("mneg_ready")
        ln_var = sem("ln_var")
        ln_rstd = sem("ln_rstd")
        ln_coef = sem("ln_coef")
        h_ready = sem("h_ready")
        deg_ok = sem("deg_ok")
        parts_ready = sem("parts_ready")
        parts_out = sem("parts_out")
        stacked = sem("stacked")
        shift_out = sem("shift_out")
        ones_row = sem("ones_row")
        shift_in = sem("shift_in")
        m0_ready = sem("m0_ready")
        pm_ready = sem("pm_ready")
        pm_used = sem("pm_used")
        mixed = sem("mixed")
        drep_ready = sem("drep_ready")
        weights = sem("weights")
        tile_used = sem("tile_used")
        f2_part = sem("f2_part")
        f2_max = sem("f2_max")
        f2_mid = sem("f2_mid")
        tjdj = sem("tjdj")
        amrep_ready = sem("amrep_ready")
        d_ready = sem("d_ready")
        k_ready = sem("k_ready")
        hb_ready = sem("hb_ready")
        elu_ready = sem("elu_ready")
        elu_sum = sem("elu_sum")

        N_W = 20
        block = ctx.enter_context(nc.Block())

        def wait_full(eng, b, *key):
            u, n = uses[key]
            eng.wait_ge(full[u], b * count[u] + n + 1)
            return U[u]

        def wait_free(b, *key):
            u, n = uses[key]
            nc.tensor.wait_ge(free[u], b * count[u] + n + 1)
            return U[u]

        def wait_read(eng, b, *key):
            u, n = uses[key]
            eng.wait_ge(free[u], b * count[u] + n + 2)

        def apart(eng):
            eng.sem_inc(passed, 1)

        def freed(ins, *key):
            return ins.then_inc(free[uses[key][0]], 1)

        def filled(ins, *key):
            return ins.then_inc(full[uses[key][0]], 1)

        adj_v = adj.rearrange("b (t p) m -> b t p m", p=P)
        x_v = x_in.rearrange("b (t p) d -> b p t d", p=P)
        out_v = out.rearrange("b (t p) d -> b p t d", p=P)

        def row(ap):
            return ap.partition_broadcast(P)


        @block.sync
        def _(sp):
            n = 0

            def load(dst, src):
                nonlocal n
                n += 1
                sp.dma_start(dst, src).then_inc(w_in, 16)

            load(w1[:, :], W1)
            load(w2[:, :, :], W2.rearrange("(c p) n -> p c n", p=P))
            for c in range(C1):
                load(b1c[:, c:c + 1], b1[c * P:(c + 1) * P].unsqueeze(1))
            load(b2r[:, :], row(b2))
            load(bgr[:, :], row(bg))
            for i, w in enumerate((Wg, Wq, Wk, Wv, Wo)):
                load(wnat[:, i, :], w)
            load(w3[:, :, :], W3.rearrange("h f o -> f h o"))
            load(b3r[:, :, :].rearrange("p h o -> p (h o)"), row(bias3.rearrange("h o -> (h o)")))
            load(w3v[:, 0, :, :].rearrange("p h o -> p (h o)"), row(w31.rearrange("h o -> (h o)")))
            load(w3v[:, 1, :, :].rearrange("p h o -> p (h o)"), row(w32.rearrange("h o -> (h o)")))
            load(epsc, row(eps0))
            load(wec, row(We.rearrange("h o -> (h o)")))
            load(b31c, row(b31))
            load(b32c, row(b32))
            load(alc, row(alpha))
            assert n == N_W
            def load_adj(b, t):
                sp.dma_start(adjN[:, t % AR, :], adj_v[bass.ds(b, 1), t].rearrange("a p m -> (a p) m")).then_inc(adj_in[t % AR], 16)

            def load_x(b):
                sp.dma_start(xin[:, :, :], x_v[bass.ds(b, 1)].rearrange("a p t d -> (a p) t d")).then_inc(x_loaded, 16)

            def through_layer_2(b):
                for t in range(AR, T):
                    sp.wait_ge(adj_sum, b * T + t - AR + 1)
                    apart(sp)
                    wait_full(sp, b, "adjT", t - AR)
                    apart(sp)
                    load_adj(b, t)
                for s in range(2):
                    sp.wait_ge(parts_ready, b * 2 + s + 1)
                    sp.dma_start(scratch[s].rearrange("k r n -> r k n"), parts[:, s, :, :]).then_inc(parts_out, 16)
                sp.wait_ge(parts_out, b * 32 + 32)
                for s, dst in ((0, qs), (1, ks)):
                    src = scratch[s].rearrange("k (h d) n -> k d h n", h=H)
                    order = (0, 0, 0, 1, 1, 2) if s == 0 else (0, 1, 2, 0, 1, 0)
                    for i, k in enumerate(order):
                        sp.dma_start(dst[i * HD:(i + 1) * HD, :, :], src[k]).then_inc(stacked, 16)
                wait_read(sp, b, "maxT")
                sp.dma_start(shifts.rearrange("(k p) -> k p", p=P), mrow[:, :]).then_inc(shift_out, 16)
                sp.wait_ge(shift_out, b * 16 + 16)
                sp.dma_start(qs[KS:KS + 1, :, :].rearrange("a h n -> a (h n)"),
                             shifts.unsqueeze(0)).then_inc(shift_in, 16)

            def store(b):
                sp.wait_ge(x_final, b * T + T)
                apart(sp)
                sp.dma_start(out_v[bass.ds(b, 1)].rearrange("a p t d -> (a p) t d"), x[:, :, :]).then_inc(x_stored, 16)

            load_x(0)
            for t in range(AR):
                load_adj(0, t)
            with sp.Fori(0, NB - 1) as b:
                through_layer_2(b)
                sp.wait_ge(x_taken, b + 1)
                apart(sp)
                load_x(b + 1)
                sp.wait_ge(adj_sum, b * T + T)
                apart(sp)
                for t in range(AR):
                    wait_full(sp, b, "adjT", T - AR + t)
                    apart(sp)
                    load_adj(b + 1, t)
                store(b)
            through_layer_2(NB - 1)
            store(NB - 1)
            sp.wait_ge(x_stored, NB * 16)

        @block.gpsimd
        def _(pool):
            own = 0

            nc.gpsimd.memset(ident[:, :], 0.0).then_inc(setup_pool, 1)
            nc.gpsimd.memset(ones[:, :], 1.0).then_inc(setup_pool, 1)
            nc.gpsimd.memset(mhalf, -0.5).then_inc(setup_pool, 1)
            pool.wait_ge(setup_pool, 3)
            nc.gpsimd.affine_select(out=ident[:, :], in_=ident[:, :], compare_op=ALU.not_equal, fill=1.0,
                                    base=0, pattern=[[-1, P]], channel_multiplier=1).then_inc(setup_pool, 1)
            pool.wait_ge(setup_pool, 4)
            pool.wait_ge(w_in, 16 * N_W)

            with pool.Fori(0, NB) as b:
                def norm(k):
                    pool.wait_ge(ln_var, b * 4 + k + 1)
                    nc.gpsimd.tensor_tensor(rstd, ve, mhalf, ALU.pow).then_inc(ln_rstd, 1)

                pool.wait_ge(x_loaded, b * 16 + 16)
                nc.gpsimd.tensor_tensor(x[:, :, :], xin[:, :, :], b2r[:, :].unsqueeze(1).to_broadcast([P, T, P]), ALU.add).then_inc(x_based, 1)
                norm(0)
                pool.wait_ge(ln_rstd, b * 4 + 1)
                pool.wait_ge(x_based, b + 1)
                apart(pool)
                nc.gpsimd.memset(ks[KS:KS + 1, :, :], 1.0).then_inc(ones_row, 1)
                pool.wait_ge(ones_row, b + 1)
                pool.wait_ge(deg_ok, b * 2 + 1)
                nc.gpsimd.tensor_tensor(dpos, degc, mhalf, ALU.pow).then_inc(deg_ok, 1)
                norm(1)
                norm(2)
                for j in range(T):
                    pool.wait_ge(m0_ready, b * T + j + 1)
                    if j >= 2:
                        pool.wait_ge(pm_used, b * T + j - 1)
                    s = (j % 2) * 2 * N
                    nc.gpsimd.tensor_tensor(pm[:, s:s + N], m0[:, :], adjT[:, j, :], ALU.add)
                    nc.gpsimd.tensor_tensor(pm[:, s + N:s + 2 * N], m0[:, :], adjT[:, j, :], ALU.subtract).then_inc(pm_ready, 1)
                norm(3)
                pool.wait_ge(f2_part, b + 1)
                apart(pool)
                nc.gpsimd.partition_all_reduce(f2x, f2p, P, bass.bass_isa.ReduceOp.max).then_inc(f2_max, 1)
                pool.wait_ge(h_ready, b * 4 * T + 4 * T)
                pool.wait_ge(pm_used, b * T + T)
                for t in range(T):
                    nc.gpsimd.tensor_tensor(hb[:, t, :].rearrange("p (h d) -> p h d", h=H3), b3r[:, :, :],
                                            hN[:, t, :].unsqueeze(1).to_broadcast([P, H3, P]), ALU.add).then_inc(hb_ready, 1)
                for t in range(T):
                    o = 3 * (t % 2)
                    pool.wait_ge(elu_ready, b * T + t + 1)
                    nc.gpsimd.tensor_tensor(tail[:, o, :], tail[:, o + 1, :], tail[:, o + 2, :], ALU.add).then_inc(pool_own, 1)
                    pool.wait_ge(pool_own, b * 2 * T + 2 * t + 1)
                    nc.gpsimd.tensor_tensor(tail[:, o, 0:2 * P], tail[:, o, 0:2 * P], tail[:, o, 2 * P:4 * P], ALU.add).then_inc(pool_own, 1)
                    pool.wait_ge(pool_own, b * 2 * T + 2 * t + 2)
                    nc.gpsimd.tensor_tensor(tail[:, o, 0:P], tail[:, o, 0:P], tail[:, o, P:2 * P], ALU.add).then_inc(elu_sum, 1)
                pool.wait_ge(x_stored, b * 16 + 16)

        @block.scalar
        def _(act):
            act.wait_ge(w_in, 16 * N_W)
            act.wait_ge(setup_pe, 1)
            nc.scalar.activation(wT[:, :, :].rearrange("p k o -> p (k o)"), U[0][:, 0:5 * P], ACT.Copy).then_inc(setup_pe, 1)

            with act.Fori(0, NB) as b:
                def normalise(k, src):
                    act.wait_ge(ln_coef, b * 4 + k + 1)
                    for t in range(T):
                        nc.scalar.activation(hN[:, t, :], src[:, t, :], ACT.Relu, bias=nm[:, t:t + 1],
                                             scale=rstd[:, t:t + 1]).then_inc(h_ready, 1)

                act.wait_ge(x_loaded, b * 16 + 16)
                normalise(0, xin)
                act.wait_ge(h_ready, b * 4 * T + T)
                act.wait_ge(x_based, b + 1)
                act.sem_inc(x_taken, 1)
                for t in range(T):
                    if t % 2 == 0:
                        u = wait_full(act, b, "adjT", t)
                        freed(nc.scalar.activation(adjT[:, :, t * P:(t + 1) * P], u[:, :].rearrange("p (m n) -> p m n", m=T),
                                                   ACT.Copy), "adjT", t)
                    act.wait_ge(adj_max, b * T + t + 1)
                    nc.scalar.activation(tmpT[:, :], adjN[:, t % AR, :], ACT.Copy, accum_out=asum[:, t:t + 1]).then_inc(act_own, 1)
                    act.wait_ge(act_own, b * T + t + 1)
                    nc.scalar.activation(tmpT[:, :], adjN[:, t % AR, :], ACT.Exp, bias=namax[:, t:t + 1],
                                         accum_out=esum[:, t:t + 1]).then_inc(adj_sum, 1)
                    act.wait_ge(adj_sum, b * T + t + 1)

                def to_sbuf(dst, *key):
                    u = wait_full(act, b, *key)
                    freed(nc.scalar.activation(dst, u[:, :], ACT.Copy), *key)

                to_sbuf(tmpT[:, :], "agg", 0)
                for c in range(C1):
                    u = wait_full(act, b, "hid", c)
                    freed(nc.scalar.activation(hid[:, c, :], u[:, :], ACT.Relu, bias=b1c[:, c:c + 1]), "hid", c)
                normalise(1, x)
                to_sbuf(tmpT[:, :], "agg", 1)
                normalise(2, x)
                to_sbuf(hT[:, :], "hT", 2)
                u = wait_full(act, b, "q")
                freed(nc.scalar.activation(tmpT[:, :], u[:, :], ACT.Copy, scale=SCALE), "q")
                u = wait_full(act, b, "k")
                act.wait_ge(parts_ready, b * 2 + 1)
                freed(nc.scalar.activation(tmpT[:, :], u[:, :], ACT.Copy), "k")
                u = wait_full(act, b, "v")
                nc.scalar.activation(va[:, :, :, HD:32], ones[:, 0:1].unsqueeze(1).unsqueeze(1).to_broadcast([P, T, H, 32 - HD]), ACT.Copy)
                freed(nc.scalar.activation(va[:, :, :, 0:HD], u[:, :].rearrange("p (t h d) -> p t h d", t=T, h=H), ACT.Copy), "v")
                u = wait_full(act, b, "maxT")
                freed(nc.scalar.activation(mrow[:, :], u[0:H * T, 0:P], ACT.Copy), "maxT")
                for n in range(T * H):
                    wait_read(act, b, "score", n // H, n % H)
                    nc.scalar.activation(ring[:, n % RING, :], ring[:, n % RING, :], ACT.Exp).then_inc(weights, 1)
                for g, dst in ((0, tmpT), (1, hT)):
                    to_sbuf(dst[:, :], "pv", g)
                to_sbuf(hT[:, :], "oT")
                normalise(3, x)
                to_sbuf(hT[:, :], "hT", 3)
                act.wait_ge(f2_mid, b + 1)
                nc.scalar.activation(tj[:, :, :], f2m[:, :, :], ACT.Exp, scale=1.0 - LEAK)
                nc.scalar.activation(dj[:, :, :], f2m[:, :, :], ACT.Exp, scale=LEAK).then_inc(tjdj, 1)
                for h in range(H3):
                    u = wait_full(act, b, "f1", h)
                    freed(nc.scalar.activation(rho[:, h, :], u[:, :], ACT.Exp, bias=cb[:, h:h + 1],
                                               scale=-(1.0 - LEAK)), "f1", h)
                for j in range(T):
                    if j == T - 1:
                        wait_read(act, b, "amax")
                    else:
                        act.wait_ge(d_ready, b * (T - 1) + j + 1)
                    n = T * H + j
                    act.wait_ge(tile_used, b * (T * H + T + T * H3) + n - RING + 1)
                    nc.scalar.activation(ring[:, n % RING, :], adjT[:, j, :], ACT.Exp).then_inc(weights, 1)
                    act.wait_ge(weights, b * (T * H + T) + n + 1)
                    nc.scalar.activation(adjT[:, j, :], adjT[:, j, :], ACT.Exp, scale=PENALTY).then_inc(k_ready, 1)
                to_sbuf(tmpT[:, :], "ca")
                for h in range(H3):
                    u = wait_full(act, b, "num", h)
                    freed(nc.scalar.activation(numT[:, h, :], u[:, :], ACT.Copy), "num", h)
                    u = wait_full(act, b, "den", h)
                    freed(nc.scalar.activation(denS[:, h, :], u[:, 0:HALF], ACT.Copy), "den", h)
                for t in range(T):
                    o = 3 * (t % 2)
                    wait_read(act, b, "tail", t)
                    if t >= 2:
                        act.wait_ge(elu_sum, b * T + t - 1)
                    nc.scalar.activation(tail[:, o + 1, :], tail[:, o, :], ACT.Relu, scale=-1.0).then_inc(relu_neg, 1)
                    act.wait_ge(relu_neg, b * T + t + 1)
                    nc.scalar.activation(tail[:, o + 1, :], tail[:, o + 1, :], ACT.Exp, scale=-1.0)
                    nc.scalar.activation(tail[:, o + 2, :], tail[:, o, :], ACT.Relu).then_inc(elu_ready, 1)

        @block.tensor
        def _(pe):
            for i in range(4):
                pe.sem_inc(free[i], 1)
            pe.wait_ge(setup_pool, 4)
            pe.wait_ge(w_in, 16 * N_W)
            for i in range(5):
                last = pe.transpose(U[0][:, i * P:(i + 1) * P], wnat[:, i, :], ident[:, :])
            last.then_inc(setup_pe, 1)
            pe.wait_ge(setup_pe, 2)
            pe.wait_ge(setup_dve, 3)

            with pe.Fori(0, NB) as b:
                def halves(u, lhsT, rhs):
                    for i in range(NH):
                        last = pe.matmul(u[:, i * HALF:(i + 1) * HALF], lhsT, rhs[:, i * HALF:(i + 1) * HALF], start=True, stop=True)
                    return last

                def aggregate(i, diag):
                    u = wait_free(b, "agg", i)
                    pe.wait_ge(h_ready, b * 4 * T + (i + 1) * T)
                    for half in range(NH):
                        for m in range(T):
                            last = pe.matmul(u[:, half * HALF:(half + 1) * HALF], hN[:, m, :],
                                             adjT[:, m, half * HALF:(half + 1) * HALF], start=(m == 0), stop=(m == T - 1))
                            if m == 0:
                                for n in range(half * T // NH, (half + 1) * T // NH):
                                    pe.matmul(u[:, n * P:(n + 1) * P], hN[:, n, :], diag, start=False, stop=False,
                                              skip_group_check=True)
                    filled(last, "agg", i)

                def node_rows(lhs, weights_T, *key):
                    u = wait_free(b, *key)
                    for t in range(T):
                        last = pe.matmul(u[:, t * P:(t + 1) * P], lhs[:, t * P:(t + 1) * P], weights_T, start=True, stop=True)
                    filled(last, *key)

                def features_up(k, *key):
                    u = wait_free(b, *key)
                    pe.wait_ge(h_ready, b * 4 * T + k * T + T)
                    for t in range(T):
                        last = pe.transpose(u[:, t * P:(t + 1) * P], hN[:, t, :], ident[:, :])
                    filled(last, *key)

                def made(*key):
                    wait_read(pe, b, *key)

                for t in range(T):
                    u = wait_free(b, "adjT", t)
                    pe.wait_ge(adj_in[t % AR], b * 16 * (T // AR) + 16 * (t // AR) + 16)
                    for m in range(T):
                        last = pe.transpose(u[:, m * P:(m + 1) * P], adjN[:, t % AR, m * P:(m + 1) * P], ident[:, :])
                    filled(last, "adjT", t)
                for t in range(T - 4, T):
                    made("adjT", t)
                aggregate(0, identE[:, :])
                made("agg", 0)
                for c in range(C1):
                    u = wait_free(b, "hid", c)
                    filled(halves(u, w1[:, c * P:(c + 1) * P], tmpT), "hid", c)
                for c in range(C1):
                    made("hid", c)
                u = wait_free(b, "mlp")
                for t in range(T):
                    for c in range(C1):
                        last = pe.matmul(u[:, t * P:(t + 1) * P], hid[:, c, t * P:(t + 1) * P], w2[:, c, :], start=(c == 0), stop=(c == C1 - 1))
                filled(last, "mlp")
                aggregate(1, ident[:, :])
                made("agg", 1)
                node_rows(tmpT, wT[:, 0, :], "lin1")
                features_up(2, "hT", 2)
                made("hT", 2)
                u = wait_free(b, "q")
                filled(halves(u, wT[:, 1, :], hT), "q")
                u = wait_free(b, "k")
                filled(halves(u, wT[:, 2, :], hT), "k")
                node_rows(hT, wT[:, 3, :], "v")
                pe.wait_ge(stacked, b * 192 + 192)
                for h in range(H):
                    for t in range(T):
                        u = wait_free(b, "max", h, t)
                        for i in range(NH):
                            last = pe.matmul(u[:, i * HALF:(i + 1) * HALF], qs[0:KS, h, t * P:(t + 1) * P],
                                             ks[0:KS, h, i * HALF:(i + 1) * HALF], start=True, stop=True)
                        filled(last, "max", h, t)
                u = wait_free(b, "maxT")
                pe.wait_ge(mneg_ready, b + 1)
                apart(pe)
                filled(pe.transpose(u[0:H * T, 0:P], mneg[:, :, :].rearrange("p h t -> p (h t)"), ident[:, :]), "maxT")
                pe.wait_ge(shift_in, b * 16 + 16)
                pe.wait_ge(ones_row, b + 1)
                made("v")
                pv = [wait_free(b, "pv", g) for g in range(2)]

                def attend(j, g):
                    pe.wait_ge(weights, b * (T * H + T) + j * H + 4 * g + 4)
                    for half in range(NH):
                        for h4 in range(4):
                            h = 4 * g + h4
                            last = pe.matmul(pv[g][32 * h4:32 * h4 + 32, half * HALF:(half + 1) * HALF], va[:, j, h, :],
                                             ring[:, (j * H + h) % RING, half * HALF:(half + 1) * HALF],
                                             start=(j == 0), stop=(j == T - 1), tile_position=(0, 32 * h4), skip_group_check=True)
                    last.then_inc(tile_used, 4)
                    return last

                for j in range(T):
                    for g in range(2):
                        for h in range(4 * g, 4 * g + 4):
                            u = wait_free(b, "score", j, h)
                            for i in range(NH):
                                last = pe.matmul(u[:, i * HALF:(i + 1) * HALF], ks[0:KS + 1, h, j * P:(j + 1) * P],
                                                 qs[0:KS + 1, h, i * HALF:(i + 1) * HALF], start=True, stop=True)
                            filled(last, "score", j, h)
                        if (j, g) != (0, 0):
                            attend(*((j, 0) if g else (j - 1, 1)))
                attend(T - 1, 1)
                pe.wait_ge(tile_used, b * (T * H + T + T * H3) + T * H)
                pe.sem_inc(full[uses["pv", 0][0]], 1)
                pe.sem_inc(full[uses["pv", 1][0]], 1)
                for g, src in ((0, tmpT), (1, hT)):
                    u = wait_free(b, "oN", g)
                    made("pv", g)
                    for t in range(T):
                        last = pe.transpose(u[:, t * P:(t + 1) * P], src[:, t * P:(t + 1) * P], ident[:, :])
                    filled(last, "oN", g)
                u = wait_free(b, "oT")
                made("oN", 0)
                made("oN", 1)
                for t in range(T):
                    last = pe.transpose(u[:, t * P:(t + 1) * P], hN[:, t, :], ident[:, :])
                filled(last, "oT")
                made("oT")
                node_rows(hT, wT[:, 4, :], "wo")
                features_up(3, "hT", 3)
                made("hT", 3)
                node_rows_small = wait_free(b, "f2")
                for t in range(T):
                    last = pe.matmul(node_rows_small[:, t * H3:(t + 1) * H3], hT[:, t * P:(t + 1) * P], u12[:, 1, :], start=True, stop=True)
                filled(last, "f2")
                u = wait_free(b, "amax")
                pe.wait_ge(amrep_ready, b + 1)
                for t in range(T):
                    last = pe.transpose(u[:, t * P:(t + 1) * P], m0[:, t * P:(t + 1) * P], ident[:, :])
                filled(last, "amax")
                for h in range(H3):
                    u = wait_free(b, "f1", h)
                    filled(halves(u, u1rep[:, h, :], hT), "f1", h)
                for t in range(T):
                    u = wait_free(b, "fts", t)
                    filled(pe.matmul(u[:, 0:H3 * P], hT[:, t * P:(t + 1) * P], w3[:, :, :].rearrange("p h o -> p (h o)"), start=True, stop=True), "fts", t)
                u = wait_free(b, "ca")
                for j in range(T):
                    n = T * H + j
                    pe.wait_ge(weights, b * (T * H + T) + n + 1)
                    for half in range(NH):
                        last = pe.matmul(u[:, half * HALF:(half + 1) * HALF], hN[:, j, :], ring[:, n % RING, half * HALF:(half + 1) * HALF],
                                         start=(j == 0), stop=(j == T - 1), skip_group_check=True)
                    last.then_inc(tile_used, 1)
                pe.wait_ge(tile_used, b * (T * H + T + T * H3) + T * H + T)
                pe.sem_inc(full[uses[("ca",)][0]], 1)
                pe.wait_ge(drep_ready, b + 1)
                made("fts", T - 2)
                made("fts", T - 1)
                for h in range(H3):
                    u = wait_free(b, "num", h)
                    d = wait_free(b, "den", h)
                    for j in range(T):
                        n = T * H + T + h * T + j
                        pe.wait_ge(mixed, b * T * H3 + h * T + j + 1)
                        for half in range(NH):
                            last = pe.matmul(u[:, half * HALF:(half + 1) * HALF], vals[:, j, h, :],
                                             ring[:, n % RING, half * HALF:(half + 1) * HALF],
                                             start=(j == 0), stop=(j == T - 1), skip_group_check=True)
                        if j == T - 1:
                            filled(last, "num", h)
                        if j % 2:
                            for par in range(2):
                                for half in range(NH):
                                    c = 32 * (par * NH + half)
                                    last = pe.matmul(d[c:c + 32, 0:HALF], drep[:, j - 1 + par, h, :],
                                                     ring[:, (n - 1 + par) % RING, half * HALF:(half + 1) * HALF],
                                                     start=(j == 1), stop=(j == T - 1), tile_position=(0, c), skip_group_check=True)
                            last.then_inc(tile_used, 2)
                    pe.wait_ge(tile_used, b * (T * H + T + T * H3) + T * H + T + (h + 1) * T)
                    pe.sem_inc(full[uses["den", h][0]], 1)
                u = wait_free(b, "denT")
                for h in range(H3):
                    made("num", h)
                    made("den", h)
                for h in range(H3):
                    for c in range(HALF // P):
                        k = h * (HALF // P) + c
                        last = pe.matmul(u[:, k * 4:k * 4 + 4], denS[:, h, c * P:(c + 1) * P], ident[:, 0:P:32], start=True, stop=True)
                filled(last, "denT")
                for t in range(T):
                    u = wait_free(b, "tail", t)
                    for h in range(H3):
                        pe.transpose(u[:, h * P:(h + 1) * P], numT[:, h, t * P:(t + 1) * P], ident[:, :])
                    if t == 0:
                        made("ca")
                    filled(pe.matmul(u[:, HALF:2 * HALF], tmpT[:, t * P:(t + 1) * P], w3[:, :, :].rearrange("p h o -> p (h o)"), start=True, stop=True), "tail", t)

        @block.vector
        def _(dve):
            V = nc.vector
            k = [0]

            def setup(ins):
                k[0] += 1
                ins.then_inc(dve_own, 1)
                dve.wait_ge(dve_own, k[0])

            dve.wait_ge(w_in, 16 * N_W)
            dve.wait_ge(setup_pool, 4)
            setup(V.tensor_scalar(oneE, epsc, 1.0, None, ALU.add))
            setup(V.tensor_scalar(identE[:, :], ident[:, :], oneE, None, ALU.mult))
            setup(V.tensor_scalar(wneg, wec, -1.0, None, ALU.mult))
            setup(V.tensor_tensor(wabs, wec, wneg, ALU.max))
            setup(V.tensor_scalar(wabs, wabs, TINY, None, ALU.max))
            setup(V.tensor_scalar(wpos, wec, 0.0, None, ALU.max))
            setup(V.tensor_scalar(signf[:, :], wec, 0.0, float(N), ALU.is_lt, ALU.mult))
            setup(V.tensor_copy(signi[:, :], signf[:, :]))
            setup(V.tensor_scalar(oma, alc, -1.0, 1.0, ALU.mult, ALU.add))
            for i in range(2):
                setup(V.tensor_tensor(utmp[:, :, :], w3[:, :, :], w3v[:, i, :, :], ALU.mult))
                setup(V.tensor_reduce(u12[:, i, :], utmp[:, :, :], AX.X, ALU.add))
            for h in range(H3):
                setup(V.tensor_scalar(u1rep[:, h, :], ones[:, :], u12[:, 0, h:h + 1], None, ALU.mult))
            dve.sem_inc(setup_dve, 3)
            SET = k[0]
            sign = [dve.value_load(signi[0:1, h:h + 1], min_val=0, max_val=N) for h in range(H)]

            with dve.Fori(0, NB) as b:
                c = [0]

                def own(ins):
                    c[0] += 1
                    ins.then_inc(dve_own, 1)
                    dve.wait_ge(dve_own, b * OWN + SET + c[0])

                def own_freed(ins, *key):
                    freed(ins, *key)
                    wait_read(dve, b, *key)

                def layer_norm(i, src, with_degree=False):
                    for t in range(T):
                        last = V.bn_stats(st[:, t, :], src[:, t, :])
                    own(last)
                    apart(dve)
                    for t in range(T):
                        last = V.bn_aggr(mv[:, t, :], st[:, t, :])
                    own(last)
                    V.tensor_scalar(ve, mv[:, :, 1], LN_EPS, None, ALU.add).then_inc(ln_var, 1)
                    dve.wait_ge(ln_rstd, b * 4 + i + 1)
                    if with_degree:
                        own(V.tensor_tensor(rstd, rstd, dinv, ALU.mult))
                    V.scalar_tensor_tensor(nm, mv[:, :, 0], -1.0, rstd, ALU.mult, ALU.mult).then_inc(ln_coef, 1)

                dve.wait_ge(x_loaded, b * 16 + 16)
                layer_norm(0, xin)
                for t in range(T):
                    dve.wait_ge(adj_in[t % AR], b * 16 * (T // AR) + 16 * (t // AR) + 16)
                    own(V.tensor_reduce(amax[:, t:t + 1], adjN[:, t % AR, :], AX.X, ALU.max))
                    V.tensor_scalar(maskN[:, t, :], adjN[:, t % AR, :], 0.0, MASKED, ALU.is_equal, ALU.mult)
                    V.tensor_scalar(namax[:, t:t + 1], amax[:, t:t + 1], -1.0, None, ALU.mult).then_inc(adj_max, 1)
                    if t % 2:
                        u = wait_full(dve, b, "adjT", t)
                        freed(V.tensor_copy(adjT[:, :, t * P:(t + 1) * P], u[:, :].rearrange("p (m n) -> p m n", m=T))
                              , "adjT", t)
                dve.wait_ge(adj_sum, b * T + T)
                own(V.tensor_scalar(deg, asum, 1.0, None, ALU.add))
                V.tensor_scalar(degc, deg, 1e-30, None, ALU.max).then_inc(deg_ok, 1)
                dve.wait_ge(deg_ok, b * 2 + 2)
                own(V.tensor_scalar(deg, deg, 0.0, None, ALU.is_gt))
                own(V.tensor_tensor(dinv, deg, dpos, ALU.mult))
                own(V.reciprocal(re, esum))

                def all_nodes(u):
                    return u[:, :].rearrange("p (t d) -> p t d", t=T)

                u = wait_full(dve, b, "mlp")
                dve.wait_ge(x_based, b + 1)
                ins = V.tensor_tensor(x[:, :, :], x[:, :, :], all_nodes(u), ALU.add)
                own_freed(ins, "mlp")
                layer_norm(1, x, with_degree=True)
                u = wait_full(dve, b, "lin1")
                ins = V.tensor_tensor(hN[:, :, :], all_nodes(u), dinv.unsqueeze(2).to_broadcast([P, T, P]), ALU.mult)
                own_freed(ins, "lin1")
                own(V.tensor_tensor(hN[:, :, :], hN[:, :, :], bgr[:, :].unsqueeze(1).to_broadcast([P, T, P]), ALU.add))
                own(V.scalar_tensor_tensor(x[:, :, :], hN[:, :, :], 0.0, x[:, :, :], ALU.max, ALU.add))
                layer_norm(2, x)
                for s in range(2):
                    wait_read(dve, b, "q" if s == 0 else "k")
                    own(V.tensor_copy(parts[:, s, 0, :], tmpT[:, :]))
                    own(V.tensor_tensor(tmpT[:, :], tmpT[:, :], parts[:, s, 0, :], ALU.subtract))
                    own(V.tensor_copy(parts[:, s, 1, :], tmpT[:, :]))
                    V.tensor_tensor(parts[:, s, 2, :], tmpT[:, :], parts[:, s, 1, :], ALU.subtract).then_inc(parts_ready, 1)
                for h in range(H):
                    for t in range(T):
                        u = wait_full(dve, b, "max", h, t)
                        apart(dve)
                        freed(V.tensor_tensor_reduce(u[:, :], u[:, :], maskN[:, t, :], 1.0, 3.0 * MASKED, ALU.add, ALU.max,
                                                     mx[:, h, t:t + 1]), "max", h, t)
                for t in range(T - 4, T):
                    wait_read(dve, b, "max", H - 1, t)
                own(V.tensor_tensor(mneg[:, :, :], wpos.unsqueeze(2).to_broadcast([P, H, T]),
                                    amax.unsqueeze(1).to_broadcast([P, H, T]), ALU.mult))
                own(V.tensor_tensor(mneg[:, :, :], mneg[:, :, :], mx[:, :, :], ALU.add))
                V.tensor_scalar(mneg[:, :, :], mneg[:, :, :], -1.0, None, ALU.mult).then_inc(mneg_ready, 1)

                def mask_T(j):
                    if j:
                        dve.wait_ge(pm_ready, b * T + j)
                    V.tensor_scalar(m0[:, :], adjT[:, j, :], 0.0, MASKED, ALU.is_equal, ALU.mult).then_inc(m0_ready, 1)

                mask_T(0)
                for j in range(T):
                    dve.wait_ge(pm_ready, b * T + j + 1)
                    for h in range(H):
                        n = j * H + h
                        u = wait_full(dve, b, "score", j, h)
                        if n >= RING:
                            dve.wait_ge(tile_used, b * (T * H + T + T * H3) + n - RING + 1)
                        ins = V.scalar_tensor_tensor(ring[:, n % RING, :], pm[:, bass.ds(sign[h] + (j % 2) * 2 * N, N)],
                                                     wabs[:, h:h + 1], u[:, :], ALU.mult, ALU.add)
                        freed(ins, "score", j, h)
                        if h == 0 and j + 1 < T:
                            mask_T(j + 1)
                    wait_read(dve, b, "score", j, H - 2)
                    wait_read(dve, b, "score", j, H - 1)
                    dve.sem_inc(pm_used, 1)
                for g in range(2):
                    u = wait_full(dve, b, "oN", g)
                    o4 = u[:, :].rearrange("p (t h d) -> p t h d", t=T, h=4)
                    own(V.reciprocal(rden[:, :, :], o4[:, :, :, HD]))
                    for hh in range(4):
                        ins = V.tensor_tensor(hN[:, :, (g * 4 + hh) * HD:(g * 4 + hh + 1) * HD], o4[:, :, hh, 0:HD],
                                              rden[:, :, hh].unsqueeze(2).to_broadcast([P, T, HD]), ALU.mult)
                    own_freed(ins, "oN", g)
                u = wait_full(dve, b, "wo")
                own_freed(V.tensor_tensor(x[:, :, :], x[:, :, :], all_nodes(u), ALU.add), "wo")
                layer_norm(3, x)
                V.tensor_copy(m0[:, :].rearrange("p (t d) -> p t d", t=T), amax.unsqueeze(2).to_broadcast([P, T, P])).then_inc(amrep_ready, 1)
                u = wait_full(dve, b, "f2")
                own_freed(V.tensor_tensor(f2[:, :, :], u[:, 0:T * H3].rearrange("p (t h) -> p t h", t=T),
                                          b32c.unsqueeze(1).to_broadcast([P, T, H3]), ALU.add), "f2")
                V.tensor_reduce(f2p, f2[:, :, :].rearrange("p t h -> p h t"), AX.X, ALU.max).then_inc(f2_part, 1)
                dve.wait_ge(f2_max, b + 1)
                own(V.tensor_tensor(cb, b31c, f2x, ALU.add))
                own(V.tensor_scalar(cb, cb, -(1.0 - LEAK), None, ALU.mult))
                V.tensor_tensor(f2m[:, :, :], f2[:, :, :], f2x.unsqueeze(1).to_broadcast([P, T, H3]), ALU.subtract).then_inc(f2_mid, 1)
                u = wait_full(dve, b, "amax")
                for j in range(T):
                    ins = V.tensor_tensor(adjT[:, j, :], adjT[:, j, :], u[:, :], ALU.subtract)
                    if j < T - 1:
                        ins.then_inc(d_ready, 1)
                freed(ins, "amax")
                dve.wait_ge(tjdj, b + 1)
                V.tensor_copy(drep[:, :, :, :], dj[:, :, :].unsqueeze(3).to_broadcast([P, T, H3, 32])).then_inc(drep_ready, 1)
                for t in range(T):
                    u = wait_full(dve, b, "fts", t)
                    freed(V.tensor_tensor(vals[:, t, :, :], u[:, 0:H3 * P].rearrange("p (h d) -> p h d", h=H3),
                                          dj[:, t, :].unsqueeze(2).to_broadcast([P, H3, P]), ALU.mult), "fts", t)
                for h in range(H3):
                    wait_read(dve, b, "f1", h)
                    own(V.tensor_scalar(rho[:, h, :], rho[:, h, :], 1.0, None, ALU.min))
                    for j in range(T):
                        if h == 0:
                            dve.wait_ge(k_ready, b * T + j + 1)
                        n = T * H + T + h * T + j
                        dve.wait_ge(tile_used, b * (T * H + T + T * H3) + n - RING + 1)
                        V.scalar_tensor_tensor(ring[:, n % RING, :], rho[:, h, :], tj[:, j, h:h + 1], adjT[:, j, :],
                                               ALU.max, ALU.mult).then_inc(mixed, 1)
                u = wait_full(dve, b, "denT")
                d4 = u[:, 0:16 * H3].rearrange("p (h c g) -> p h c g", h=H3, g=4)
                for half in range(NH):
                    own(V.tensor_copy(den[:, :, half * 4:half * 4 + 4], d4[:, :, :, half]))
                    ins = V.tensor_tensor(den[:, :, half * 4:half * 4 + 4], den[:, :, half * 4:half * 4 + 4], d4[:, :, :, NH + half], ALU.add)
                own_freed(ins, "denT")
                own(V.reciprocal(r1[:, :, :], den[:, :, :]))
                own(V.tensor_tensor(r1[:, :, :], r1[:, :, :], alc.unsqueeze(2).to_broadcast([P, H3, T]), ALU.mult))
                own(V.tensor_tensor(r2[:, :, :], oma.unsqueeze(2).to_broadcast([P, H3, T]), re.unsqueeze(1).to_broadcast([P, H3, T]), ALU.mult))

                def finish(t):
                    o = 3 * (t % 2)
                    dve.wait_ge(elu_sum, b * T + t + 1)
                    own(V.tensor_scalar(tail[:, o, 0:P], tail[:, o, 0:P], 1.0 / H3, -1.0, ALU.mult, ALU.add))
                    V.tensor_tensor(x[:, t, :], x[:, t, :], tail[:, o, 0:P], ALU.add).then_inc(x_final, 1)

                for t in range(T):
                    o = 3 * (t % 2)
                    u = wait_full(dve, b, "tail", t)
                    dve.wait_ge(hb_ready, b * T + t + 1)
                    if t >= 2:
                        finish(t - 2)
                        dve.wait_ge(x_final, b * T + t - 1)
                    for h in range(H3):
                        ins = V.scalar_tensor_tensor(tail[:, o, h * P:(h + 1) * P], u[:, h * P:(h + 1) * P], r1[:, h, t:t + 1],
                                                     hb[:, t, h * P:(h + 1) * P], ALU.mult, ALU.add)
                    own(ins)
                    for h in range(H3):
                        ins = V.scalar_tensor_tensor(tail[:, o, h * P:(h + 1) * P], u[:, HALF + h * P:HALF + (h + 1) * P], r2[:, h, t:t + 1],
                                                     tail[:, o, h * P:(h + 1) * P], ALU.mult, ALU.add)
                    freed(ins, "tail", t)
                finish(T - 2)
                finish(T - 1)
                assert c[0] == OWN, c[0]


_INS = ['x', 'adj', 'L0_gnn_eps', 'L0_gnn_W1', 'L0_gnn_b1', 'L0_gnn_W2', 'L0_gnn_b2', 'L1_gnn_W', 'L1_gnn_b',
        'L2_gnn_W_q', 'L2_gnn_W_k', 'L2_gnn_W_v', 'L2_gnn_W_e', 'L2_gnn_W_o', 'L3_gnn_W', 'L3_gnn_w1', 'L3_gnn_b1',
        'L3_gnn_w2', 'L3_gnn_b2', 'L3_gnn_alpha', 'L3_gnn_bias']


def kernel(**inputs):
    import numpy as _np
    import concourse.bacc as _bacc
    from concourse import mybir as _mybir
    from concourse.bass_utils import run_bass_kernel_spmd as _run

    nc = _bacc.Bacc("TRN2", target_bir_lowering=False, num_devices=1)
    arrays, args = {}, []
    for name in _INS:
        a = _np.ascontiguousarray(inputs[name])
        arrays[f"in_{name}"] = a
        args.append(nc.dram_tensor(f"in_{name}", a.shape, _mybir.dt.from_np(a.dtype), kind="ExternalInput").ap())
    shape = inputs['x'].shape
    out = nc.dram_tensor("out_x", shape, _mybir.dt.float32, kind="ExternalOutput").ap()
    scratch = nc.dram_tensor("scratch_qk_parts", (2, 3, shape[2], shape[1]), _mybir.dt.bfloat16, kind="Internal").ap()
    shifts = nc.dram_tensor("scratch_shifts", (inputs['L2_gnn_W_e'].shape[0] * shape[1],), _mybir.dt.bfloat16, kind="Internal").ap()
    graph_layers(nc, *args, out, scratch, shifts)
    r = _run(nc, [arrays], core_ids=[0])
    return r.results[0]["out_x"]
```

```python
from contextlib import ExitStack

import numpy as np

import concourse.bass as bass
from concourse import mybir

F32 = mybir.dt.float32
BF16 = mybir.dt.bfloat16
I32 = mybir.dt.int32
ALU = mybir.AluOpType
ACT = mybir.ActivationFunctionType
AX = mybir.AxisListType

P = 128
MASKED = -1.0e30
PENALTY = 1.0e9
LN_EPS = 1e-5
TINY = 1e-20
LEAK = 0.2


def graph_layers(nc, x_in, adj, eps0, W1, b1, W2, b2, Wg, bg, Wq, Wk, Wv, We, Wo,
                 W3, w31, b31, w32, b32, alpha, bias3, out, scratch, shifts):
    NB, N, D = x_in.shape
    T = N // P
    C1 = W1.shape[1] // P
    H = We.shape[0]
    HD = D // H
    H3 = W3.shape[0]
    HALF = 512
    NH = N // HALF
    PARTS = 3
    KS = 6 * HD
    RING = 8
    SCALE = float(HD) ** -0.5
    assert D == P and C1 * P == W1.shape[1] and NH == 2 and (T * H + T + T * H3) % RING == 0 and H == 8 and T == 8

    HT = T // 2
    TILES = T * H + T + T * H3

    uses, count = {}, [0] * 4

    def use(unit, *key):
        uses[key] = (unit, count[unit])
        count[unit] += 1

    for t in range(T):
        use(t % 2, "adjT", t)
    use(0, "agg", 0)
    use(1, "hid", 0)
    use(0, "hid", 1)
    use(1, "mlp", 0)
    use(0, "mlp", 1)
    use(1, "agg", 1)
    use(0, "lin1", 0)
    use(1, "lin1", 1)
    use(2, "hT", 2)
    use(3, "q")
    use(0, "k")
    use(1, "v")
    for h in range(H):
        for t in range(T):
            use((h * T + t + 2) % 4, "max", h, t)
        if h == 4:
            use(2, "maxT", 0)
    use(3, "maxT", 1)
    use(2, "pv", 0)
    use(3, "pv", 1)
    for j in range(T):
        for h in range(H):
            use(h % 2, "score", j, h)
    for g in range(2):
        use(g, "oN", g)
    use(2, "oT")
    use(3, "wo", 0)
    use(0, "wo", 1)
    use(1, "hT", 3)
    use(2, "f2")
    use(3, "amax")
    use(0, "f1", 0)
    use(1, "f1", 1)
    use(2, "ca")
    for t in range(T):
        use(t % 2, "fts", t)
    for h in range(H3):
        use(h % 2, "num", h)
        use(2, "den", h)
        if h:
            use(3, "denT", h - 1)
        if h + 2 < H3:
            use(3, "f1", h + 2)
    use(3, "denT", H3 - 1)
    for t in range(T):
        use(2 + t % 2, "tail", t)

    with ExitStack() as ctx:
        def sb(name, shape, dt=F32):
            return ctx.enter_context(nc.sbuf_tensor(name, shape, dt))

        def sem(name):
            return ctx.enter_context(nc.semaphore(name))

        U = [ctx.enter_context(nc.psum_tensor(f"U{i}", [P, N], F32)) for i in range(4)]

        ident = sb("ident", [P, P])
        identE = sb("identE", [P, P])
        w1 = sb("w1", [P, C1 * P])
        w2 = sb("w2", [P, C1, P])
        b1c = sb("b1c", [P, C1])
        b2r = sb("b2r", [P, P])
        bgr = sb("bgr", [P, P])
        wT = sb("wT", [P, 5, P])
        w3 = sb("w3", [P, H3, P])
        b3r = sb("b3r", [P, H3, P])
        u12 = sb("u12", [P, 2, H3])
        u1rep = sb("u1rep", [P, H3, P])
        col = sb("col", [P, 64])
        epsc, wec, b31c, b32c, alc = col[:, 0:1], col[:, 1:1 + H], col[:, 10:10 + H3], col[:, 14:14 + H3], col[:, 18:18 + H3]
        oneE, one, wabs, wpos, oma, mhalf = col[:, 22:23], col[:, 23:24], col[:, 24:24 + H], col[:, 32:32 + H], col[:, 40:40 + H3], col[:, 48:48 + T]
        wneg = col[:, 56:56 + H]
        signf = sb("signf", [P, H])
        signi = sb("signi", [P, H], I32)

        adjN = sb("adjN", [P, T, N])
        adjT = sb("adjT", [P, T, N])
        pm = sb("pm", [P, 2 * 2 * N])
        hb = pm[:, :].rearrange("p (t c) -> p t c", t=T)
        m0 = sb("m0", [P, N])
        stacks = sb("stacks", [P, 2 * H * N], BF16)
        qs = stacks[:, 0:H * N].rearrange("p (h n) -> p h n", h=H)
        ks = stacks[:, H * N:].rearrange("p (h n) -> p h n", h=H)
        s32 = stacks[:, :].bitcast(F32)
        vals = s32[:, 0:T * H3 * P].rearrange("p (t h d) -> p t h d", t=T, h=H3)
        numT = s32[:, T * H3 * P:].rearrange("p (h n) -> p h n", h=H3)
        ring = sb("ring", [P, RING, N])
        hid = ring[:, 0:C1, :]
        flat = ring[:, :, :].rearrange("p k n -> p (k n)")
        wnat = flat[:, 0:5 * P].rearrange("p (k d) -> p k d", k=5)
        w3v = flat[:, N:2 * N].rearrange("p (k h d) -> p k h d", k=2, h=H3)
        utmp = flat[:, 2 * N:2 * N + H3 * P].rearrange("p (h d) -> p h d", h=H3)
        misc = sb("misc", [P, 3 * N])
        parts = misc[:, :].bitcast(BF16).rearrange("p (s k n) -> p s k n", s=2, k=PARTS)
        rho = misc[:, 0:2 * N].rearrange("p (h n) -> p h n", h=2)
        tail = misc[:, :].rearrange("p (k c) -> p k c", c=HALF)
        va = sb("va", [P, T, H, 32])
        denS = va[:, :, :, :].rearrange("p t h c -> p (t h c)").rearrange("p (h n) -> p h n", h=H3)
        xin = sb("xin", [P, T, P])
        x = sb("x", [P, T, P])
        hN = sb("hN", [P, T, P])
        hT = sb("hT", [P, N])
        tmpT = sb("tmpT", [P, N])
        caT = sb("caT", [P, N])
        drep = m0[:, :].rearrange("p (t h c) -> p t h c", t=T, h=H3)
        st = sb("st", [P, T, 6])
        mv = sb("mv", [P, T, 2])
        stat = sb("stat", [P, 12, T])
        amax, namax, asum, esum, ve, rstd, nm, deg, dinv, dpos, degc, re = [stat[:, i, :] for i in range(12)]
        mx = sb("mx", [P, H, T])
        mneg = sb("mneg", [P, H, T])
        mrow = sb("mrow", [4 * T, 2, P], BF16)
        rden = sb("rden", [P, T, H // 2])
        f2 = sb("f2", [P, T, H3])
        f2m = sb("f2m", [P, T, H3])
        tj = sb("tj", [P, T, H3])
        dj = sb("dj", [P, T, H3])
        sm3 = sb("sm3", [P, 3, H3])
        f2p, f2x, cb = sm3[:, 0, :], sm3[:, 1, :], sm3[:, 2, :]
        den = sb("den", [P, H3, T])
        r1 = sb("r1", [P, H3, T])
        r2 = sb("r2", [P, H3, T])

        w_in = sem("w_in")
        setup_pool = sem("setup_pool")
        setup_dve = sem("setup_dve")
        setup_pe = sem("setup_pe")
        adj_in = [sem(f"adj_in{i}") for i in range(T)]
        adj_max = sem("adj_max")
        adj_sum = sem("adj_sum")
        plain_sum = sem("plain_sum")
        x_loaded = sem("x_loaded")
        x_taken = sem("x_taken")
        x_based = sem("x_based")
        x_stored = sem("x_stored")
        x_final = sem("x_final")
        full = [sem(f"full{i}") for i in range(4)]
        free = [sem(f"free{i}") for i in range(4)]
        own_stats = sem("own_stats")
        own_main = sem("own_main")
        own_tail = sem("own_tail")
        elu_part = sem("elu_part")
        passed = sem("passed")
        relu_neg = sem("relu_neg")
        mneg_ready = sem("mneg_ready")
        ln_var = sem("ln_var")
        ln_rstd = sem("ln_rstd")
        ln_coef = sem("ln_coef")
        h_ready = sem("h_ready")
        deg_ok = sem("deg_ok")
        parts_own = sem("parts_own")
        parts_ready = sem("parts_ready")
        parts_out = sem("parts_out")
        stacked0 = sem("stacked0")
        stacked = sem("stacked")
        shift_out = sem("shift_out")
        shift_in = [sem(f"shift_in{c}") for c in range(2)]
        ones_row = sem("ones_row")
        m0_ready = sem("m0_ready")
        pm_ready = sem("pm_ready")
        pm_used = sem("pm_used")
        mixed = sem("mixed")
        drep_ready = sem("drep_ready")
        weights = sem("weights")
        tile_used = sem("tile_used")
        f2_part = sem("f2_part")
        f2_max = sem("f2_max")
        f2_mid = sem("f2_mid")
        tjdj = sem("tjdj")
        amrep_ready = sem("amrep_ready")
        d_ready = sem("d_ready")
        k_ready = sem("k_ready")
        hb_ready = sem("hb_ready")
        elu_ready = sem("elu_ready")
        elu_sum = sem("elu_sum")

        N_W = 20
        OWN_STATS, OWN_MAIN, OWN_TAIL = 4 + T + 4, 37, 2 * T
        block = ctx.enter_context(nc.Block())

        def wait_full(eng, b, *key):
            u, n = uses[key]
            eng.wait_ge(full[u], b * count[u] + n + 1)
            return U[u]

        def wait_free(b, *key):
            u, n = uses[key]
            nc.tensor.wait_ge(free[u], b * count[u] + n + 1)
            return U[u]

        def wait_read(eng, b, *key):
            u, n = uses[key]
            eng.wait_ge(free[u], b * count[u] + n + 2)

        def apart(eng):
            eng.sem_inc(passed, 1)

        def freed(ins, *key):
            return ins.then_inc(free[uses[key][0]], 1)

        def filled(ins, *key):
            return ins.then_inc(full[uses[key][0]], 1)

        adj_v = adj.rearrange("b (t p) m -> b t p m", p=P)
        x_v = x_in.rearrange("b (t p) d -> b p t d", p=P)
        out_v = out.rearrange("b (t p) d -> b p t d", p=P)

        def row(ap):
            return ap.partition_broadcast(P)

        def graphs(eng, prologue, main, between, epilogue):
            prologue()
            with eng.Fori(0, NB - 1) as b:
                main(b, True)
                between(b)
            main(NB - 1, False)
            epilogue(NB - 1)

        BETWEEN = [("adjT", 0), ("adjT", 1), ("tail", 0), ("adjT", 2), ("adjT", 3), ("tail", 1), ("adjT", 4), ("adjT", 5),
                   ("tail", 2), ("adjT", 6), ("adjT", 7)]
        for i in range(T):
            BETWEEN.append(("agg", i))
            if 3 + i < T:
                BETWEEN.append(("tail", 3 + i))

        @block.sync
        def _(sp):
            n = 0

            def load(dst, src):
                nonlocal n
                n += 1
                sp.dma_start(dst, src).then_inc(w_in, 16)

            def load_adj(b):
                for t in range(T):
                    sp.dma_start(adjN[:, t, :], adj_v[bass.ds(b, 1), t].rearrange("a p m -> (a p) m")).then_inc(adj_in[t], 16)

            def load_x(b):
                sp.dma_start(xin[:, :, :], x_v[bass.ds(b, 1)].rearrange("a p t d -> (a p) t d")).then_inc(x_loaded, 16)

            load_x(0)
            load_adj(0)
            load(w1[:, :], W1)
            load(w2[:, :, :], W2.rearrange("(c p) n -> p c n", p=P))
            for c in range(C1):
                load(b1c[:, c:c + 1], b1[c * P:(c + 1) * P].unsqueeze(1))
            load(b2r[:, :], row(b2))
            load(bgr[:, :], row(bg))
            for i, w in enumerate((Wg, Wq, Wk, Wv, Wo)):
                load(wnat[:, i, :], w)
            load(w3[:, :, :], W3.rearrange("h f o -> f h o"))
            load(b3r[:, :, :].rearrange("p h o -> p (h o)"), row(bias3.rearrange("h o -> (h o)")))
            load(w3v[:, 0, :, :].rearrange("p h o -> p (h o)"), row(w31.rearrange("h o -> (h o)")))
            load(w3v[:, 1, :, :].rearrange("p h o -> p (h o)"), row(w32.rearrange("h o -> (h o)")))
            load(epsc, row(eps0))
            load(wec, row(We.rearrange("h o -> (h o)")))
            load(b31c, row(b31))
            load(b32c, row(b32))
            load(alc, row(alpha))
            assert n == N_W

            def main(b, more):
                for s, (name, dst) in enumerate((("q", qs), ("k", ks))):
                    wait_read(sp, b, name)
                    for h in range(H):
                        sp.dma_start(dst[0:HD, h, :], parts[h * HD:(h + 1) * HD, s, 0, :]).then_inc(stacked0, 16)
                for s in range(2):
                    sp.wait_ge(parts_ready, b * 2 + s + 1)
                    sp.dma_start(scratch[s].rearrange("k r n -> r k n"), parts[:, s, :, :]).then_inc(parts_out, 16)
                sp.wait_ge(parts_out, b * 32 + 32)
                for s, dst in ((0, qs), (1, ks)):
                    src = scratch[s].rearrange("k (h d) n -> k d h n", h=H)
                    order = (0, 0, 0, 1, 1, 2) if s == 0 else (0, 1, 2, 0, 1, 0)
                    for i, k in enumerate(order):
                        if i:
                            sp.dma_start(dst[i * HD:(i + 1) * HD, :, :], src[k]).then_inc(stacked, 16)
                for c in range(2):
                    wait_read(sp, b, "maxT", c)
                    sp.dma_start(shifts[c * 4 * N:(c + 1) * 4 * N].rearrange("(k p) -> k p", p=P), mrow[:, c, :]).then_inc(shift_out, 16)
                    sp.wait_ge(shift_out, b * 32 + 16 * c + 16)
                    sp.dma_start(qs[KS:KS + 1, 4 * c:4 * c + 4, :].rearrange("a h n -> a (h n)"),
                                 shifts[c * 4 * N:(c + 1) * 4 * N].unsqueeze(0)).then_inc(shift_in[c], 16)
                if more:
                    for t in range(T - 4, T):
                        wait_read(sp, b, "max", H - 1, t)
                        apart(sp)
                    load_adj(b + 1)
                    sp.wait_ge(x_taken, b + 1)
                    apart(sp)
                    load_x(b + 1)

            def store(b):
                sp.wait_ge(x_final, b * T + T)
                apart(sp)
                sp.dma_start(out_v[bass.ds(b, 1)].rearrange("a p t d -> (a p) t d"), hb[:, :, 0:P]).then_inc(x_stored, 16)

            graphs(sp, lambda: None, main, store, store)
            sp.wait_ge(x_stored, NB * 16)

        @block.gpsimd
        def _(pool):
            nc.gpsimd.memset(ident[:, :], 0.0).then_inc(setup_pool, 1)
            nc.gpsimd.memset(one, 1.0).then_inc(setup_pool, 1)
            nc.gpsimd.memset(mhalf, -0.5).then_inc(setup_pool, 1)
            pool.wait_ge(setup_pool, 3)
            nc.gpsimd.affine_select(out=ident[:, :], in_=ident[:, :], compare_op=ALU.not_equal, fill=1.0,
                                    base=0, pattern=[[-1, P]], channel_multiplier=1).then_inc(setup_pool, 1)
            pool.wait_ge(setup_pool, 4)
            pool.wait_ge(w_in, 16 * N_W)

            def norm(b, k):
                for half in range(2):
                    c = slice(half * HT, half * HT + HT)
                    pool.wait_ge(ln_var, b * 8 + 2 * k + half + 1)
                    nc.gpsimd.tensor_tensor(rstd[:, c], ve[:, c], mhalf[:, c], ALU.pow).then_inc(ln_rstd, 1)

            def stats(b):
                norm(b, 0)
                pool.wait_ge(deg_ok, b * 2 + 1)
                nc.gpsimd.tensor_tensor(dpos, degc, mhalf, ALU.pow).then_inc(deg_ok, 1)

            def start(b):
                pool.wait_ge(x_loaded, b * 16 + 16)
                nc.gpsimd.tensor_tensor(x[:, :, :], xin[:, :, :], b2r[:, :].unsqueeze(1).to_broadcast([P, T, P]), ALU.add).then_inc(x_based, 1)
                pool.wait_ge(x_based, b + 1)
                pool.wait_ge(deg_ok, b * 2 + 2)
                apart(pool)
                nc.gpsimd.memset(ks[KS:KS + 1, :, :], 1.0).then_inc(ones_row, 1)
                pool.wait_ge(ones_row, b + 1)

            def main(b, more):
                norm(b, 1)
                norm(b, 2)
                for s, (name, src) in enumerate((("q", tmpT), ("k", m0))):
                    wait_read(pool, b, name)
                    nc.gpsimd.tensor_tensor(src[:, :], src[:, :], parts[:, s, 0, :], ALU.subtract).then_inc(parts_own, 1)
                    pool.wait_ge(parts_own, b * 4 + 2 * s + 1)
                    apart(pool)
                    nc.gpsimd.tensor_copy(parts[:, s, 1, :], src[:, :]).then_inc(parts_own, 1)
                    pool.wait_ge(parts_own, b * 4 + 2 * s + 2)
                    nc.gpsimd.tensor_tensor(parts[:, s, 2, :], src[:, :], parts[:, s, 1, :], ALU.subtract).then_inc(parts_ready, 1)
                for j in range(T):
                    pool.wait_ge(m0_ready, b * T + j + 1)
                    if j >= 2:
                        pool.wait_ge(pm_used, b * T + j - 1)
                    s = (j % 2) * 2 * N
                    nc.gpsimd.tensor_tensor(pm[:, s:s + N], m0[:, :], adjT[:, j, :], ALU.add)
                    nc.gpsimd.tensor_tensor(pm[:, s + N:s + 2 * N], m0[:, :], adjT[:, j, :], ALU.subtract).then_inc(pm_ready, 1)
                norm(b, 3)
                pool.wait_ge(f2_part, b + 1)
                apart(pool)
                nc.gpsimd.partition_all_reduce(f2x, f2p, P, bass.bass_isa.ReduceOp.max).then_inc(f2_max, 1)
                pool.wait_ge(h_ready, b * 4 * T + 4 * T)
                pool.wait_ge(pm_used, b * T + T)
                for t in range(T):
                    nc.gpsimd.tensor_tensor(hb[:, t, :].rearrange("p (h d) -> p h d", h=H3), b3r[:, :, :],
                                            hN[:, t, :].unsqueeze(1).to_broadcast([P, H3, P]), ALU.add).then_inc(hb_ready, 1)
                if more:
                    stats(b + 1)

            def elu_sums(b, t):
                o = 3 * (t % 2)
                pool.wait_ge(elu_ready, b * T + t + 1)
                nc.gpsimd.tensor_tensor(tail[:, o, :], tail[:, o + 1, :], tail[:, o + 2, :], ALU.add).then_inc(elu_part, 1)
                pool.wait_ge(elu_part, b * 2 * T + 2 * t + 1)
                nc.gpsimd.tensor_tensor(tail[:, o, 0:2 * P], tail[:, o, 0:2 * P], tail[:, o, 2 * P:4 * P], ALU.add).then_inc(elu_part, 1)
                pool.wait_ge(elu_part, b * 2 * T + 2 * t + 2)
                nc.gpsimd.tensor_tensor(tail[:, o, 0:P], tail[:, o, 0:P], tail[:, o, P:2 * P], ALU.add).then_inc(elu_sum, 1)

            def between(b):
                for t in range(T):
                    elu_sums(b, t)
                pool.wait_ge(x_final, b * T + T)
                pool.wait_ge(x_stored, b * 16 + 16)
                start(b + 1)

            def prologue():
                stats(0)
                start(0)

            graphs(pool, prologue, main, between, lambda b: [elu_sums(b, t) for t in range(T)])

        @block.scalar
        def _(act):
            act.wait_ge(w_in, 16 * N_W)
            act.wait_ge(setup_pe, 1)
            nc.scalar.activation(wT[:, :, :].rearrange("p k o -> p (k o)"), U[0][:, 0:5 * P], ACT.Copy).then_inc(setup_pe, 1)

            def normalise(b, k, src):
                for t in range(T):
                    if t % HT == 0:
                        act.wait_ge(ln_coef, b * 8 + 2 * k + t // HT + 1)
                    nc.scalar.activation(hN[:, t, :], src[:, t, :], ACT.Relu, bias=nm[:, t:t + 1],
                                         scale=rstd[:, t:t + 1]).then_inc(h_ready, 1)

            def sums(b, t):
                act.wait_ge(adj_max, b * T + t + 1)
                nc.scalar.activation(hT[:, :], adjN[:, t, :], ACT.Copy, accum_out=asum[:, t:t + 1]).then_inc(plain_sum, 1)
                act.wait_ge(plain_sum, b * T + t + 1)
                nc.scalar.activation(hT[:, :], adjN[:, t, :], ACT.Exp, bias=namax[:, t:t + 1],
                                     accum_out=esum[:, t:t + 1]).then_inc(adj_sum, 1)
                act.wait_ge(adj_sum, b * T + t + 1)

            def adj_turned(b, t):
                if t % 2 == 0:
                    u = wait_full(act, b, "adjT", t)
                    freed(nc.scalar.activation(adjT[:, :, t * P:(t + 1) * P], u[:, :].rearrange("p (m n) -> p m n", m=T),
                                               ACT.Copy), "adjT", t)

            def to_sbuf(b, dst, *key):
                u = wait_full(act, b, *key)
                freed(nc.scalar.activation(dst, u[:, :], ACT.Copy), *key)

            def layer_0(b):
                to_sbuf(b, tmpT[:, :], "agg", 0)
                for c in range(C1):
                    u = wait_full(act, b, "hid", c)
                    freed(nc.scalar.activation(hid[:, c, :], u[:, :], ACT.Relu, bias=b1c[:, c:c + 1]), "hid", c)
                act.wait_ge(x_based, b + 1)
                act.sem_inc(x_taken, 1)

            def exp_rho(b, h):
                u = wait_full(act, b, "f1", h)
                if h >= 2:
                    act.wait_ge(mixed, b * T * H3 + (h - 1) * T)
                freed(nc.scalar.activation(rho[:, h % 2, :], u[:, :], ACT.Exp, bias=cb[:, h:h + 1],
                                           scale=-(1.0 - LEAK)), "f1", h)

            def main(b, more):
                normalise(b, 1, x)
                to_sbuf(b, tmpT[:, :], "agg", 1)
                normalise(b, 2, x)
                to_sbuf(b, hT[:, :], "hT", 2)
                u = wait_full(act, b, "q")
                nc.scalar.activation(parts[:, 0, 0, :], u[:, :], ACT.Copy, scale=SCALE)
                freed(nc.scalar.activation(tmpT[:, :], u[:, :], ACT.Copy, scale=SCALE), "q")
                u = wait_full(act, b, "v")
                nc.scalar.activation(va[:, :, :, HD:32], one.unsqueeze(1).unsqueeze(1).to_broadcast([P, T, H, 32 - HD]), ACT.Copy)
                freed(nc.scalar.activation(va[:, :, :, 0:HD], u[:, :].rearrange("p (t h d) -> p t h d", t=T, h=H), ACT.Copy), "v")
                for c in range(2):
                    u = wait_full(act, b, "maxT", c)
                    freed(nc.scalar.activation(mrow[:, c, :], u[0:4 * T, 0:P], ACT.Copy), "maxT", c)
                for n in range(T * H):
                    wait_read(act, b, "score", n // H, n % H)
                    nc.scalar.activation(ring[:, n % RING, :], ring[:, n % RING, :], ACT.Exp).then_inc(weights, 1)
                for g, dst in ((0, tmpT), (1, hT)):
                    to_sbuf(b, dst[:, :], "pv", g)
                to_sbuf(b, hT[:, :], "oT")
                normalise(b, 3, x)
                to_sbuf(b, hT[:, :], "hT", 3)
                act.wait_ge(f2_mid, b + 1)
                nc.scalar.activation(tj[:, :, :], f2m[:, :, :], ACT.Exp, scale=1.0 - LEAK)
                nc.scalar.activation(dj[:, :, :], f2m[:, :, :], ACT.Exp, scale=LEAK).then_inc(tjdj, 1)
                exp_rho(b, 0)
                exp_rho(b, 1)
                for j in range(T):
                    if j == T - 1:
                        wait_read(act, b, "amax")
                    else:
                        act.wait_ge(d_ready, b * (T - 1) + j + 1)
                    n = T * H + j
                    act.wait_ge(tile_used, b * TILES + n - RING + 1)
                    nc.scalar.activation(ring[:, n % RING, :], adjT[:, j, :], ACT.Exp).then_inc(weights, 1)
                    act.wait_ge(weights, b * (T * H + T) + n + 1)
                    nc.scalar.activation(adjT[:, j, :], adjT[:, j, :], ACT.Exp, scale=PENALTY).then_inc(k_ready, 1)
                to_sbuf(b, caT[:, :], "ca")
                for h in range(H3):
                    if more and h == 1:
                        wait_full(act, b, "f1", H3 - 1)
                        for t in range(T // 2):
                            sums(b + 1, t)
                    if more and h == 2:
                        for t in range(T // 2, T):
                            sums(b + 1, t)
                    if more and h == 3:
                        normalise(b + 1, 0, xin)
                    to_sbuf(b, numT[:, h, :], "num", h)
                    u = wait_full(act, b, "den", h)
                    freed(nc.scalar.activation(denS[:, h, :], u[:, 0:HALF], ACT.Copy), "den", h)
                    if h + 2 < H3:
                        exp_rho(b, h + 2)

            def elus(b, t):
                o = 3 * (t % 2)
                wait_read(act, b, "tail", t)
                if t >= 2:
                    act.wait_ge(elu_sum, b * T + t - 1)
                nc.scalar.activation(tail[:, o + 1, :], tail[:, o, :], ACT.Relu, scale=-1.0).then_inc(relu_neg, 1)
                act.wait_ge(relu_neg, b * T + t + 1)
                nc.scalar.activation(tail[:, o + 1, :], tail[:, o + 1, :], ACT.Exp, scale=-1.0)
                nc.scalar.activation(tail[:, o + 2, :], tail[:, o, :], ACT.Relu).then_inc(elu_ready, 1)

            def between(b):
                for what, t in BETWEEN:
                    if what == "tail":
                        elus(b, t)
                    elif what == "adjT":
                        adj_turned(b + 1, t)
                layer_0(b + 1)

            def prologue():
                for t in range(T):
                    sums(0, t)
                normalise(0, 0, xin)
                for t in range(T):
                    adj_turned(0, t)
                layer_0(0)

            graphs(act, prologue, main, between, lambda b: [elus(b, t) for t in range(T)])

        @block.tensor
        def _(pe):
            for i in range(4):
                pe.sem_inc(free[i], 1)
            pe.wait_ge(setup_pool, 4)
            pe.wait_ge(w_in, 16 * N_W)
            for i in range(5):
                last = pe.transpose(U[0][:, i * P:(i + 1) * P], wnat[:, i, :], ident[:, :])
            last.then_inc(setup_pe, 1)
            pe.wait_ge(setup_pe, 2)
            pe.wait_ge(setup_dve, 3)
            w3_all = w3[:, :, :].rearrange("p h o -> p (h o)")

            def half(ap, i):
                return ap[:, i * HALF:(i + 1) * HALF]

            def halves(u, lhsT, rhs):
                for i in range(NH):
                    last = pe.matmul(half(u, i), lhsT, half(rhs, i), start=True, stop=True)
                return last

            def aggregate(b, i, m, diag):
                u = wait_free(b, "agg", i) if m == 0 else U[uses["agg", i][0]]
                pe.wait_ge(h_ready, b * 4 * T + i * T + m + 1)
                for k in range(NH):
                    pe.matmul(half(u, k), hN[:, m, :], half(adjT[:, m, :], k), start=(m == 0), stop=False, skip_group_check=True)
                last = pe.matmul(u[:, m * P:(m + 1) * P], hN[:, m, :], diag, start=False, stop=(m == T - 1), skip_group_check=True)
                if m == T - 1:
                    filled(last, "agg", i)

            def node_rows(b, lhs, weights_T, *key):
                for k in range(2):
                    u = wait_free(b, *key, k)
                    for t in range(HT):
                        n = k * HT + t
                        last = pe.matmul(u[:, t * P:(t + 1) * P], lhs[:, n * P:(n + 1) * P], weights_T, start=True, stop=True)
                    filled(last, *key, k)

            def features_up(b, k, *key):
                u = wait_free(b, *key)
                for t in range(T):
                    pe.wait_ge(h_ready, b * 4 * T + k * T + t + 1)
                    last = pe.transpose(u[:, t * P:(t + 1) * P], hN[:, t, :], ident[:, :])
                filled(last, *key)

            def made(b, *key):
                wait_read(pe, b, *key)

            def turn_adj(b, t):
                u = wait_free(b, "adjT", t)
                pe.wait_ge(adj_in[t], b * 16 + 16)
                for m in range(T):
                    last = pe.transpose(u[:, m * P:(m + 1) * P], adjN[:, t, m * P:(m + 1) * P], ident[:, :])
                filled(last, "adjT", t)

            def aggregate_0(b, m):
                if m == 0:
                    made(b, "adjT", T - 2)
                    made(b, "adjT", T - 1)
                aggregate(b, 0, m, identE[:, :])

            def layer_0(b):
                made(b, "agg", 0)
                for c in range(C1):
                    u = wait_free(b, "hid", c)
                    filled(halves(u, w1[:, c * P:(c + 1) * P], tmpT), "hid", c)
                for c in range(C1):
                    made(b, "hid", c)
                for k in range(2):
                    u = wait_free(b, "mlp", k)
                    for t in range(HT):
                        n = k * HT + t
                        for c in range(C1):
                            last = pe.matmul(u[:, t * P:(t + 1) * P], hid[:, c, n * P:(n + 1) * P], w2[:, c, :], start=(c == 0), stop=(c == C1 - 1))
                    filled(last, "mlp", k)

            def attend(b, j, g, k):
                pv = U[uses["pv", g][0]]
                if k == 0:
                    pe.wait_ge(weights, b * (T * H + T) + j * H + 4 * g + 4)
                for h4 in range(4):
                    h = 4 * g + h4
                    last = pe.matmul(pv[32 * h4:32 * h4 + 32, k * HALF:(k + 1) * HALF], va[:, j, h, :],
                                     half(ring[:, (j * H + h) % RING, :], k),
                                     start=(j == 0), stop=(j == T - 1), tile_position=(0, 32 * h4), skip_group_check=True)
                if k == 1:
                    last.then_inc(tile_used, 4)

            def sum_columns(b, h, j):
                d = wait_free(b, "den", h) if j == 1 else U[uses["den", h][0]]
                n = T * H + T + h * T + j
                for par in range(2):
                    for k in range(NH):
                        c = 32 * (par * NH + k)
                        last = pe.matmul(d[c:c + 32, 0:HALF], drep[:, j - 1 + par, h, :], half(ring[:, (n - 1 + par) % RING, :], k),
                                         start=(j == 1), stop=(j == T - 1), tile_position=(0, c), skip_group_check=True)
                last.then_inc(tile_used, 2)

            def turn_sums(b, h):
                u = wait_free(b, "denT", h)
                made(b, "den", h)
                for c in range(HALF // P):
                    last = pe.matmul(u[:, c * 4:c * 4 + 4], denS[:, h, c * P:(c + 1) * P], ident[:, 0:P:32], start=True, stop=True)
                filled(last, "denT", h)

            def f1_rows(b, h):
                u = wait_free(b, "f1", h)
                filled(halves(u, u1rep[:, h, :], hT), "f1", h)

            def main(b, more):
                for m in range(T):
                    aggregate(b, 1, m, ident[:, :])
                made(b, "agg", 1)
                node_rows(b, tmpT, wT[:, 0, :], "lin1")
                features_up(b, 2, "hT", 2)
                made(b, "hT", 2)
                u = wait_free(b, "q")
                filled(halves(u, wT[:, 1, :], hT), "q")
                u = wait_free(b, "k")
                filled(halves(u, wT[:, 2, :], hT), "k")
                u = wait_free(b, "v")
                for t in range(T):
                    last = pe.matmul(u[:, t * P:(t + 1) * P], hT[:, t * P:(t + 1) * P], wT[:, 3, :], start=True, stop=True)
                filled(last, "v")
                pe.wait_ge(stacked0, b * 32 * H + 32 * H)
                for h in range(H):
                    for t in range(T):
                        u = wait_free(b, "max", h, t)
                        filled(halves(u, qs[0:HD, h, t * P:(t + 1) * P], ks[0:HD, h, :]), "max", h, t)
                    if h == 4:
                        turn_shifts(b, 0)
                turn_shifts(b, 1)
                pe.wait_ge(stacked, b * 160 + 160)
                pe.wait_ge(ones_row, b + 1)
                made(b, "v")
                for g in range(2):
                    wait_free(b, "pv", g)
                for j in range(T):
                    for g in range(2):
                        if j == 0:
                            pe.wait_ge(shift_in[g], b * 16 + 16)
                        before = (j, 0) if g else (j - 1, 1)
                        for h4 in range(4):
                            h = 4 * g + h4
                            u = wait_free(b, "score", j, h)
                            filled(halves(u, ks[0:KS + 1, h, j * P:(j + 1) * P], qs[0:KS + 1, h, :]), "score", j, h)
                            if before[0] >= 0 and h4 >= 2:
                                attend(b, *before, h4 - 2)
                attend(b, T - 1, 1, 0)
                attend(b, T - 1, 1, 1)
                pe.wait_ge(tile_used, b * TILES + T * H)
                pe.sem_inc(full[uses["pv", 0][0]], 1)
                pe.sem_inc(full[uses["pv", 1][0]], 1)
                for g, src in ((0, tmpT), (1, hT)):
                    u = wait_free(b, "oN", g)
                    made(b, "pv", g)
                    for t in range(T):
                        last = pe.transpose(u[:, t * P:(t + 1) * P], src[:, t * P:(t + 1) * P], ident[:, :])
                    filled(last, "oN", g)
                u = wait_free(b, "oT")
                made(b, "oN", 0)
                made(b, "oN", 1)
                for t in range(T):
                    last = pe.transpose(u[:, t * P:(t + 1) * P], hN[:, t, :], ident[:, :])
                filled(last, "oT")
                made(b, "oT")
                node_rows(b, hT, wT[:, 4, :], "wo")
                features_up(b, 3, "hT", 3)
                made(b, "hT", 3)
                u = wait_free(b, "f2")
                for t in range(T):
                    last = pe.matmul(u[:, t * H3:(t + 1) * H3], hT[:, t * P:(t + 1) * P], u12[:, 1, :], start=True, stop=True)
                filled(last, "f2")
                u = wait_free(b, "amax")
                pe.wait_ge(amrep_ready, b + 1)
                for t in range(T):
                    last = pe.transpose(u[:, t * P:(t + 1) * P], m0[:, t * P:(t + 1) * P], ident[:, :])
                filled(last, "amax")
                f1_rows(b, 0)
                f1_rows(b, 1)

                def softmax_adj(j):
                    u = wait_free(b, "ca") if j == 0 else U[uses[("ca",)][0]]
                    n = T * H + j
                    pe.wait_ge(weights, b * (T * H + T) + n + 1)
                    for k in range(NH):
                        last = pe.matmul(half(u, k), hN[:, j, :], half(ring[:, n % RING, :], k), start=(j == 0), stop=(j == T - 1),
                                         skip_group_check=True)
                    last.then_inc(tile_used, 1)

                for t in range(T):
                    u = wait_free(b, "fts", t)
                    filled(pe.matmul(u[:, 0:H3 * P], hT[:, t * P:(t + 1) * P], w3_all, start=True, stop=True), "fts", t)
                    if t:
                        softmax_adj(t - 1)
                softmax_adj(T - 1)
                pe.wait_ge(tile_used, b * TILES + T * H + T)
                pe.sem_inc(full[uses[("ca",)][0]], 1)
                pe.wait_ge(drep_ready, b + 1)
                made(b, "fts", T - 2)
                made(b, "fts", T - 1)
                for h in range(H3):
                    u = wait_free(b, "num", h)
                    for j in range(T):
                        pe.wait_ge(mixed, b * T * H3 + h * T + j + 1)
                        for k in range(NH):
                            last = pe.matmul(half(u, k), vals[:, j, h, :], half(ring[:, (T * H + T + h * T + j) % RING, :], k),
                                             start=(j == 0), stop=(j == T - 1), skip_group_check=True)
                        if j == T - 1:
                            filled(last, "num", h)
                        if j % 2:
                            sum_columns(b, h, j)
                        if j == 2 and h:
                            turn_sums(b, h - 1)
                        if j == 5 and h + 2 < H3:
                            f1_rows(b, h + 2)
                    pe.wait_ge(tile_used, b * TILES + T * H + T + (h + 1) * T)
                    pe.sem_inc(full[uses["den", h][0]], 1)
                turn_sums(b, H3 - 1)

            def turn_shifts(b, c):
                u = wait_free(b, "maxT", c)
                pe.wait_ge(mneg_ready, b * 2 + c + 1)
                apart(pe)
                filled(pe.transpose(u[0:4 * T, 0:P], mneg[:, 4 * c:4 * c + 4, :].rearrange("p h t -> p (h t)"), ident[:, :]), "maxT", c)

            def finish_rows(b, t):
                u = wait_free(b, "tail", t)
                if t == 0:
                    made(b, "ca")
                    for h in range(H3):
                        made(b, "num", h)
                for h in range(H3):
                    pe.transpose(u[:, h * P:(h + 1) * P], numT[:, h, t * P:(t + 1) * P], ident[:, :])
                filled(pe.matmul(u[:, HALF:2 * HALF], caT[:, t * P:(t + 1) * P], w3_all, start=True, stop=True), "tail", t)

            def between(b):
                for what, t in BETWEEN:
                    if what == "tail":
                        finish_rows(b, t)
                    elif what == "adjT":
                        turn_adj(b + 1, t)
                    else:
                        aggregate_0(b + 1, t)
                layer_0(b + 1)

            def prologue():
                for t in range(T):
                    turn_adj(0, t)
                for m in range(T):
                    aggregate_0(0, m)
                layer_0(0)

            graphs(pe, prologue, main, between, lambda b: [finish_rows(b, t) for t in range(T)])

        @block.vector
        def _(dve):
            V = nc.vector
            k = [0]

            def setup(ins):
                k[0] += 1
                ins.then_inc(own_main, 1)
                dve.wait_ge(own_main, k[0])

            dve.wait_ge(w_in, 16 * N_W)
            dve.wait_ge(setup_pool, 4)
            setup(V.tensor_scalar(oneE, epsc, 1.0, None, ALU.add))
            setup(V.tensor_scalar(identE[:, :], ident[:, :], oneE, None, ALU.mult))
            setup(V.tensor_scalar(wneg, wec, -1.0, None, ALU.mult))
            setup(V.tensor_tensor(wabs, wec, wneg, ALU.max))
            setup(V.tensor_scalar(wabs, wabs, TINY, None, ALU.max))
            setup(V.tensor_scalar(wpos, wec, 0.0, None, ALU.max))
            setup(V.tensor_scalar(signf[:, :], wec, 0.0, float(N), ALU.is_lt, ALU.mult))
            setup(V.tensor_copy(signi[:, :], signf[:, :]))
            setup(V.tensor_scalar(oma, alc, -1.0, 1.0, ALU.mult, ALU.add))
            for i in range(2):
                setup(V.tensor_tensor(utmp[:, :, :], w3[:, :, :], w3v[:, i, :, :], ALU.mult))
                setup(V.tensor_reduce(u12[:, i, :], utmp[:, :, :], AX.X, ALU.add))
            for h in range(H3):
                setup(V.tensor_copy(u1rep[:, h, :], u12[:, 0, h:h + 1].to_broadcast([P, P])))
            dve.sem_inc(setup_dve, 3)
            SET = k[0]
            sign = [dve.value_load(signi[0:1, h:h + 1], min_val=0, max_val=N) for h in range(H)]

            chains = {"stats": (own_stats, OWN_STATS, 0),
                      "main": (own_main, OWN_MAIN, SET), "tail": (own_tail, OWN_TAIL, 0)}
            steps = {}

            def begin(b, phase):
                steps[phase] = [b, 0]

            def own(phase, ins):
                s, per_graph, base = chains[phase]
                steps[phase][1] += 1
                b, c = steps[phase]
                ins.then_inc(s, 1)
                s_at = b * per_graph + base + c
                dve.wait_ge(s, s_at)

            def end(phase):
                assert steps[phase][1] == chains[phase][1], (phase, steps[phase][1])

            def own_freed(b, ins, *key):
                freed(ins, *key)
                wait_read(dve, b, *key)

            def layer_norm(b, i, src, phase, ready=None, with_degree=False):
                for k in range(2):
                    if ready:
                        ready(k)
                    for t in range(k * HT, k * HT + HT):
                        last = V.bn_stats(st[:, t, :], src[:, t, :])
                    own(phase, last)
                    apart(dve)
                    for t in range(k * HT, k * HT + HT):
                        last = V.bn_aggr(mv[:, t, :], st[:, t, :])
                    own(phase, last)
                    c = slice(k * HT, k * HT + HT)
                    V.tensor_scalar(ve[:, c], mv[:, c, 1], LN_EPS, None, ALU.add).then_inc(ln_var, 1)
                for k in range(2):
                    c = slice(k * HT, k * HT + HT)
                    dve.wait_ge(ln_rstd, b * 8 + 2 * i + k + 1)
                    if with_degree:
                        own(phase, V.tensor_tensor(rstd[:, c], rstd[:, c], dinv[:, c], ALU.mult))
                    V.scalar_tensor_tensor(nm[:, c], mv[:, c, 0], -1.0, rstd[:, c], ALU.mult, ALU.mult).then_inc(ln_coef, 1)

            def half_nodes(u):
                return u[:, 0:HALF].rearrange("p (t d) -> p t d", t=HT)

            def adj_max_tile(b, t):
                dve.wait_ge(adj_in[t], b * 16 + 16)
                own("stats", V.tensor_reduce(amax[:, t:t + 1], adjN[:, t, :], AX.X, ALU.max))
                V.tensor_scalar(namax[:, t:t + 1], amax[:, t:t + 1], -1.0, None, ALU.mult).then_inc(adj_max, 1)

            def first_norm(b):
                dve.wait_ge(x_loaded, b * 16 + 16)
                layer_norm(b, 0, xin, "stats")

            def degrees(b):
                dve.wait_ge(adj_sum, b * T + T)
                own("stats", V.tensor_scalar(deg, asum, 1.0, None, ALU.add))
                V.tensor_scalar(degc, deg, 1e-30, None, ALU.max).then_inc(deg_ok, 1)
                dve.wait_ge(deg_ok, b * 2 + 2)
                own("stats", V.tensor_scalar(deg, deg, 0.0, None, ALU.is_gt))
                own("stats", V.tensor_tensor(dinv, deg, dpos, ALU.mult))
                own("stats", V.reciprocal(re, esum))
                end("stats")

            def adj_turned(b, t):
                if t % 2:
                    u = wait_full(dve, b, "adjT", t)
                    freed(V.tensor_copy(adjT[:, :, t * P:(t + 1) * P], u[:, :].rearrange("p (m n) -> p m n", m=T)), "adjT", t)

            def layer_0(b):
                for t in range(T):
                    wait_full(dve, b, "adjT", t)
                    V.tensor_scalar(adjN[:, t, :], adjN[:, t, :], 0.0, MASKED, ALU.is_equal, ALU.mult)
                dve.wait_ge(x_based, b + 1)
                for k in range(2):
                    u = wait_full(dve, b, "mlp", k)
                    own_x = V.tensor_tensor(x[:, k * HT:(k + 1) * HT, :], x[:, k * HT:(k + 1) * HT, :], half_nodes(u), ALU.add)
                    freed(own_x, "mlp", k)

            def main(b, more):
                begin(b, "main")
                layer_norm(b, 1, x, "main", ready=lambda k: wait_read(dve, b, "mlp", k), with_degree=True)
                for k in range(2):
                    c = slice(k * HT, (k + 1) * HT)
                    u = wait_full(dve, b, "lin1", k)
                    ins = V.tensor_tensor(hN[:, c, :], half_nodes(u), dinv[:, c].unsqueeze(2).to_broadcast([P, HT, P]), ALU.mult)
                    own_freed(b, ins, "lin1", k)
                    own("main", V.tensor_tensor(hN[:, c, :], hN[:, c, :], bgr[:, :].unsqueeze(1).to_broadcast([P, HT, P]), ALU.add))
                    own("main", V.scalar_tensor_tensor(x[:, c, :], hN[:, c, :], 0.0, x[:, c, :], ALU.max, ALU.add))
                layer_norm(b, 2, x, "main")
                u = wait_full(dve, b, "k")
                V.tensor_copy(parts[:, 1, 0, :], u[:, :])
                freed(V.tensor_copy(m0[:, :], u[:, :]), "k")
                for h in range(H):
                    for t in range(T):
                        u = wait_full(dve, b, "max", h, t)
                        apart(dve)
                        freed(V.tensor_tensor_reduce(u[:, :], u[:, :], adjN[:, t, :], 1.0, 3.0 * MASKED, ALU.add, ALU.max,
                                                     mx[:, h, t:t + 1]), "max", h, t)
                    if h % 4 == 3:
                        for t in range(T - 4, T):
                            wait_read(dve, b, "max", h, t)
                        c = slice(h - 3, h + 1)
                        own("main", V.tensor_tensor(mneg[:, c, :], wpos[:, c].unsqueeze(2).to_broadcast([P, 4, T]),
                                                    amax.unsqueeze(1).to_broadcast([P, 4, T]), ALU.mult))
                        own("main", V.tensor_tensor(mneg[:, c, :], mneg[:, c, :], mx[:, c, :], ALU.add))
                        V.tensor_scalar(mneg[:, c, :], mneg[:, c, :], -1.0, None, ALU.mult).then_inc(mneg_ready, 1)

                def mask_T(j):
                    if j:
                        dve.wait_ge(pm_ready, b * T + j)
                    else:
                        dve.wait_ge(parts_ready, b * 2 + 2)
                    V.tensor_scalar(m0[:, :], adjT[:, j, :], 0.0, MASKED, ALU.is_equal, ALU.mult).then_inc(m0_ready, 1)

                mask_T(0)
                for j in range(T):
                    dve.wait_ge(pm_ready, b * T + j + 1)
                    for h in range(H):
                        n = j * H + h
                        u = wait_full(dve, b, "score", j, h)
                        if n >= RING:
                            dve.wait_ge(tile_used, b * TILES + n - RING + 1)
                        ins = V.scalar_tensor_tensor(ring[:, n % RING, :], pm[:, bass.ds(sign[h] + (j % 2) * 2 * N, N)],
                                                     wabs[:, h:h + 1], u[:, :], ALU.mult, ALU.add)
                        freed(ins, "score", j, h)
                        if h == 0 and j + 1 < T:
                            mask_T(j + 1)
                    wait_read(dve, b, "score", j, H - 2)
                    wait_read(dve, b, "score", j, H - 1)
                    dve.sem_inc(pm_used, 1)
                dve.wait_ge(pm_ready, b * T + T)
                V.tensor_copy(m0[:, :].rearrange("p (t d) -> p t d", t=T), amax.unsqueeze(2).to_broadcast([P, T, P])).then_inc(amrep_ready, 1)
                own("main", V.tensor_tensor(r2[:, :, :], oma.unsqueeze(2).to_broadcast([P, H3, T]), re.unsqueeze(1).to_broadcast([P, H3, T]), ALU.mult))
                for g in range(2):
                    u = wait_full(dve, b, "oN", g)
                    o4 = u[:, :].rearrange("p (t h d) -> p t h d", t=T, h=4)
                    own("main", V.reciprocal(rden[:, :, :], o4[:, :, :, HD]))
                    for hh in range(4):
                        ins = V.tensor_tensor(hN[:, :, (g * 4 + hh) * HD:(g * 4 + hh + 1) * HD], o4[:, :, hh, 0:HD],
                                              rden[:, :, hh].unsqueeze(2).to_broadcast([P, T, HD]), ALU.mult)
                    own_freed(b, ins, "oN", g)

                def add_wo(k):
                    u = wait_full(dve, b, "wo", k)
                    c = slice(k * HT, (k + 1) * HT)
                    own_freed(b, V.tensor_tensor(x[:, c, :], x[:, c, :], half_nodes(u), ALU.add), "wo", k)

                layer_norm(b, 3, x, "main", ready=add_wo)
                u = wait_full(dve, b, "f2")
                own_freed(b, V.tensor_tensor(f2[:, :, :], u[:, 0:T * H3].rearrange("p (t h) -> p t h", t=T),
                                             b32c.unsqueeze(1).to_broadcast([P, T, H3]), ALU.add), "f2")
                V.tensor_reduce(f2p, f2[:, :, :].rearrange("p t h -> p h t"), AX.X, ALU.max).then_inc(f2_part, 1)
                dve.wait_ge(f2_max, b + 1)
                own("main", V.tensor_tensor(cb, b31c, f2x, ALU.add))
                own("main", V.tensor_scalar(cb, cb, -(1.0 - LEAK), None, ALU.mult))
                V.tensor_tensor(f2m[:, :, :], f2[:, :, :], f2x.unsqueeze(1).to_broadcast([P, T, H3]), ALU.subtract).then_inc(f2_mid, 1)
                am = wait_full(dve, b, "amax")
                for j in range(T):
                    ins = V.tensor_tensor(adjT[:, j, :], adjT[:, j, :], am[:, :], ALU.subtract)
                    if j < T - 1:
                        ins.then_inc(d_ready, 1)
                    else:
                        freed(ins, "amax")
                    if j == 0:
                        dve.wait_ge(tjdj, b + 1)
                    u = wait_full(dve, b, "fts", j)
                    freed(V.tensor_tensor(vals[:, j, :, :], u[:, 0:H3 * P].rearrange("p (h d) -> p h d", h=H3),
                                          dj[:, j, :].unsqueeze(2).to_broadcast([P, H3, P]), ALU.mult), "fts", j)
                V.tensor_copy(drep[:, :, :, :], dj[:, :, :].unsqueeze(3).to_broadcast([P, T, H3, 32])).then_inc(drep_ready, 1)
                if more:
                    begin(b + 1, "stats")
                for h in range(H3):
                    wait_read(dve, b, "f1", h)
                    own("main", V.tensor_scalar(rho[:, h % 2, :], rho[:, h % 2, :], 1.0, None, ALU.min))
                    for j in range(T):
                        if h == 0:
                            dve.wait_ge(k_ready, b * T + j + 1)
                        n = T * H + T + h * T + j
                        dve.wait_ge(tile_used, b * TILES + n - RING + 1)
                        V.scalar_tensor_tensor(ring[:, n % RING, :], rho[:, h % 2, :], tj[:, j, h:h + 1], adjT[:, j, :],
                                               ALU.max, ALU.mult).then_inc(mixed, 1)
                        if more and (h, j % 2) == (1, 0):
                            adj_max_tile(b + 1, j // 2)
                        if more and (h, j % 2) == (2, 0):
                            adj_max_tile(b + 1, T // 2 + j // 2)
                        if more and (h, j) == (2, T - 1):
                            first_norm(b + 1)
                        if more and (h, j) == (3, T // 2):
                            degrees(b + 1)
                    if h:
                        columns(b, h - 1)
                columns(b, H3 - 1)
                own("main", V.reciprocal(r1[:, :, :], den[:, :, :]))
                own("main", V.tensor_tensor(r1[:, :, :], r1[:, :, :], alc.unsqueeze(2).to_broadcast([P, H3, T]), ALU.mult))
                end("main")

            def columns(b, h):
                u = wait_full(dve, b, "denT", h)
                d4 = u[:, 0:16].rearrange("p (c g) -> p c g", g=4)
                for k in range(NH):
                    last = V.tensor_copy(den[:, h, k * 4:k * 4 + 4], d4[:, :, k])
                own("main", last)
                for k in range(NH):
                    last = V.tensor_tensor(den[:, h, k * 4:k * 4 + 4], den[:, h, k * 4:k * 4 + 4], d4[:, :, NH + k], ALU.add)
                own_freed(b, last, "denT", h)

            def combine(b, t):
                o = 3 * (t % 2)
                u = wait_full(dve, b, "tail", t)
                dve.wait_ge(hb_ready, b * T + t + 1)
                if t >= 2:
                    finish(b, t - 2)
                for h in range(H3):
                    ins = V.scalar_tensor_tensor(tail[:, o, h * P:(h + 1) * P], u[:, h * P:(h + 1) * P], r1[:, h, t:t + 1],
                                                 hb[:, t, h * P:(h + 1) * P], ALU.mult, ALU.add)
                own("tail", ins)
                for h in range(H3):
                    ins = V.scalar_tensor_tensor(tail[:, o, h * P:(h + 1) * P], u[:, HALF + h * P:HALF + (h + 1) * P], r2[:, h, t:t + 1],
                                                 tail[:, o, h * P:(h + 1) * P], ALU.mult, ALU.add)
                freed(ins, "tail", t)

            def finish(b, t):
                o = 3 * (t % 2)
                dve.wait_ge(elu_sum, b * T + t + 1)
                own("tail", V.tensor_scalar(tail[:, o, 0:P], tail[:, o, 0:P], 1.0 / H3, -1.0, ALU.mult, ALU.add))
                V.tensor_tensor(hb[:, t, 0:P], x[:, t, :], tail[:, o, 0:P], ALU.add).then_inc(x_final, 1)
                dve.wait_ge(x_final, b * T + t + 1)

            def between(b):
                begin(b, "tail")
                for what, t in BETWEEN:
                    if what == "tail":
                        combine(b, t)
                    elif what == "adjT":
                        adj_turned(b + 1, t)
                finish(b, T - 2)
                finish(b, T - 1)
                end("tail")
                layer_0(b + 1)

            def prologue():
                begin(0, "stats")
                for t in range(T):
                    adj_max_tile(0, t)
                first_norm(0)
                degrees(0)
                for t in range(T):
                    adj_turned(0, t)
                layer_0(0)

            def epilogue(b):
                begin(b, "tail")
                for t in range(T):
                    combine(b, t)
                finish(b, T - 2)
                finish(b, T - 1)
                end("tail")

            graphs(dve, prologue, main, between, epilogue)


_INS = ['x', 'adj', 'L0_gnn_eps', 'L0_gnn_W1', 'L0_gnn_b1', 'L0_gnn_W2', 'L0_gnn_b2', 'L1_gnn_W', 'L1_gnn_b',
        'L2_gnn_W_q', 'L2_gnn_W_k', 'L2_gnn_W_v', 'L2_gnn_W_e', 'L2_gnn_W_o', 'L3_gnn_W', 'L3_gnn_w1', 'L3_gnn_b1',
        'L3_gnn_w2', 'L3_gnn_b2', 'L3_gnn_alpha', 'L3_gnn_bias']


def kernel(**inputs):
    import numpy as _np
    import concourse.bacc as _bacc
    from concourse import mybir as _mybir
    from concourse.bass_utils import run_bass_kernel_spmd as _run

    nc = _bacc.Bacc("TRN2", target_bir_lowering=False, num_devices=1)
    arrays, args = {}, []
    for name in _INS:
        a = _np.ascontiguousarray(inputs[name])
        arrays[f"in_{name}"] = a
        args.append(nc.dram_tensor(f"in_{name}", a.shape, _mybir.dt.from_np(a.dtype), kind="ExternalInput").ap())
    shape = inputs['x'].shape
    out = nc.dram_tensor("out_x", shape, _mybir.dt.float32, kind="ExternalOutput").ap()
    scratch = nc.dram_tensor("scratch_qk_parts", (2, 3, shape[2], shape[1]), _mybir.dt.bfloat16, kind="Internal").ap()
    shifts = nc.dram_tensor("scratch_shifts", (inputs['L2_gnn_W_e'].shape[0] * shape[1],), _mybir.dt.bfloat16, kind="Internal").ap()
    graph_layers(nc, *args, out, scratch, shifts)
    r = _run(nc, [arrays], core_ids=[0])
    return r.results[0]["out_x"]
```

```python
from contextlib import ExitStack

import numpy as np

import concourse.bass as bass
from concourse import mybir

F32 = mybir.dt.float32
BF16 = mybir.dt.bfloat16
I32 = mybir.dt.int32
ALU = mybir.AluOpType
ACT = mybir.ActivationFunctionType
AX = mybir.AxisListType

P = 128
MASKED = -1.0e30
PENALTY = 1.0e9
LN_EPS = 1e-5
TINY = 1e-20
LEAK = 0.2


def graph_layers(nc, x_in, adj, eps0, W1, b1, W2, b2, Wg, bg, Wq, Wk, Wv, We, Wo,
                 W3, w31, b31, w32, b32, alpha, bias3, out, scratch, shifts):
    NB, N, D = x_in.shape
    T = N // P
    C1 = W1.shape[1] // P
    H = We.shape[0]
    HD = D // H
    H3 = W3.shape[0]
    HALF = 512
    NH = N // HALF
    PARTS = 3
    KS = 6 * HD
    RING = 8
    SCALE = float(HD) ** -0.5
    assert D == P and C1 * P == W1.shape[1] and NH == 2 and (T * H + T + T * H3) % RING == 0 and H == 8 and T == 8

    HT = T // 2
    TILES = T * H + T + T * H3

    uses, count = {}, [0] * 4

    def use(unit, *key):
        uses[key] = (unit, count[unit])
        count[unit] += 1

    for t in range(T):
        use(0, "adjT", t)
    use(0, "agg", 0)
    use(1, "hid", 0)
    use(0, "hid", 1)
    use(1, "mlp", 0)
    use(0, "mlp", 1)
    use(1, "agg", 1)
    use(0, "lin1", 0)
    use(1, "lin1", 1)
    use(2, "hT", 2)
    use(3, "q")
    use(0, "k")
    use(1, "v")
    DIRECT = 2
    MAX_ORDER = [0, 2, 3, 4, 1, 5, 6, 7]
    for h in range(H):
        for i, t in enumerate(MAX_ORDER):
            use((h * T + i + 2) % 4, "max", h, t)
        if h == 5:
            use(2, "maxT", 0)
    use(3, "maxT", 1)
    FOLDS = 6
    fold_order = []
    for h in range(H):
        fold_order += [(h - 1, 1), (h - 1, 2), (h, 0), (h - 1, 3), (h - 1, 4), (h - 1, 5)] if h else [(h, 0)]
    fold_order += [(H - 1, step) for step in range(1, FOLDS)]
    use(2, "pv", 0)
    use(3, "pv", 1)
    for j in range(T):
        for h in range(H):
            use(h % 2, "score", j, h)
    for k in range(NH):
        use(k, "oN", k)
    for k in range(NH):
        use(2 + k, "oT", k)
    for k in range(NH):
        use(k, "wo", k)
    use(3, "amax")
    use(2, "hT", 3)
    use(0, "f2")
    use(0, "f1", 0)
    use(1, "f1", 1)
    use(2, "ca")
    for t in range(T):
        use(t % 2, "fts", t)
    for h in range(H3):
        use(h % 2, "num", h)
        use(2, "den", h)
        if h:
            use(3, "denT", h - 1)
        if h + 2 < H3:
            use(3, "f1", h + 2)
    use(3, "denT", H3 - 1)
    for t in range(T):
        use(2 + t % 2, "tail", t)

    with ExitStack() as ctx:
        def sb(name, shape, dt=F32):
            return ctx.enter_context(nc.sbuf_tensor(name, shape, dt))

        def sem(name):
            return ctx.enter_context(nc.semaphore(name))

        U = [ctx.enter_context(nc.psum_tensor(f"U{i}", [P, N], F32)) for i in range(4)]

        ident = sb("ident", [P, P])
        identB = sb("identB", [P, P], BF16)
        identE = sb("identE", [P, P])
        w1 = sb("w1", [P, C1 * P])
        w2 = sb("w2", [P, C1, P])
        b1c = sb("b1c", [P, C1])
        b2r = sb("b2r", [P, P])
        bgr = sb("bgr", [P, P])
        wT = sb("wT", [P, 5, P])
        w3 = sb("w3", [P, H3, P])
        b3r = sb("b3r", [P, H3, P])
        u12 = sb("u12", [P, 2, H3])
        col = sb("col", [P, 64])
        epsc, wec, b31c, b32c, alc = col[:, 0:1], col[:, 1:1 + H], col[:, 10:10 + H3], col[:, 14:14 + H3], col[:, 18:18 + H3]
        oneE, one, wabs, wpos, oma, mhalf = col[:, 22:23], col[:, 23:24], col[:, 24:24 + H], col[:, 32:32 + H], col[:, 40:40 + H3], col[:, 48:48 + T]
        wneg = col[:, 56:56 + H]
        headm = sb("headm", [P, H])
        signf = sb("signf", [P, H])
        signi = sb("signi", [P, H], I32)

        adjN = sb("adjN", [P, T, N])
        adjB = adjN[:, :, :].rearrange("p t n -> p (t n)").bitcast(BF16).rearrange("p (t n) -> p t n", t=T)
        mask0 = sb("mask0", [P, N], BF16)
        kh = [adjB[:, h, N:2 * N] for h in range(H)]
        maskN = [mask0[:, :]] + [adjB[:, t - 1, 0:N] for t in range(1, T)]
        adjT = sb("adjT", [P, T, N])
        pm = sb("pm", [P, 2 * 2 * N])
        hb = pm[:, :].rearrange("p (t c) -> p t c", t=T)
        m0 = sb("m0", [P, N])
        stacks = sb("stacks", [P, 2 * H * N], BF16)
        qs = stacks[:, 0:H * N].rearrange("p (h n) -> p h n", h=H)
        ks = stacks[:, H * N:].rearrange("p (h n) -> p h n", h=H)
        s32 = stacks[:, :].bitcast(F32)
        vals = s32[:, 0:T * H3 * P].rearrange("p (t h d) -> p t h d", t=T, h=H3)
        numT = s32[:, T * H3 * P:].rearrange("p (h n) -> p h n", h=H3)
        ring = sb("ring", [P, RING, N])
        hid = ring[:, 0:C1, :]
        flat = ring[:, :, :].rearrange("p k n -> p (k n)")
        folds = flat.bitcast(BF16).rearrange("p (s k n) -> p s k n", s=2, k=RING)
        wnat = flat[:, 0:5 * P].rearrange("p (k d) -> p k d", k=5)
        w3v = flat[:, N:2 * N].rearrange("p (k h d) -> p k h d", k=2, h=H3)
        utmp = flat[:, 2 * N:2 * N + H3 * P].rearrange("p (h d) -> p h d", h=H3)
        misc = sb("misc", [P, 3 * N])
        parts = misc[:, :].bitcast(BF16).rearrange("p (s k n) -> p s k n", s=2, k=PARTS)
        rho = misc[:, 0:2 * N].rearrange("p (h n) -> p h n", h=2)
        tail = misc[:, :].rearrange("p (k c) -> p k c", c=HALF)
        va = sb("va", [P, T, H, 32])
        denS = va[:, :, :, :].rearrange("p t h c -> p (t h c)").rearrange("p (h n) -> p h n", h=H3)
        xin = sb("xin", [P, T, P])
        x = sb("x", [P, T, P])
        hN = sb("hN", [P, T, P])
        hT = sb("hT", [P, N])
        xs = hT[:, :].rearrange("p (t d) -> p t d", t=T)
        tmpT = sb("tmpT", [P, N])
        caT = sb("caT", [P, N])
        drep = m0[:, :].rearrange("p (t h c) -> p t h c", t=T, h=H3)
        st = sb("st", [P, T, 6])
        mv = sb("mv", [P, T, 2])
        stat = sb("stat", [P, 12, T])
        amax, namax, asum, esum, ve, rstd, nm, deg, dinv, dpos, degc, re = [stat[:, i, :] for i in range(12)]
        mx = sb("mx", [P, H, T])
        mneg = sb("mneg", [P, H, T])
        mrow = sb("mrow", [4 * T, 2, P], BF16)
        rden = sb("rden", [P, 2, T // 2, H // 2])
        f2 = sb("f2", [P, T, H3])
        f2m = sb("f2m", [P, T, H3])
        tj = sb("tj", [P, T, H3])
        dj = sb("dj", [P, T, H3])
        sm3 = sb("sm3", [P, 3, H3])
        f2p, f2x, cb = sm3[:, 0, :], sm3[:, 1, :], sm3[:, 2, :]
        den = sb("den", [P, H3, T])
        r1 = sb("r1", [P, H3, T])
        r2 = sb("r2", [P, H3, T])

        w_in = sem("w_in")
        setup_pool = sem("setup_pool")
        setup_dve = sem("setup_dve")
        setup_pe = sem("setup_pe")
        adj_in = [sem(f"adj_in{i}") for i in range(T)]
        adj_max = sem("adj_max")
        adj_sum = sem("adj_sum")
        plain_sum = sem("plain_sum")
        mask_ready = sem("mask_ready")
        x_loaded = sem("x_loaded")
        x_taken = sem("x_taken")
        x_based = sem("x_based")
        x_kept = sem("x_kept")
        x_stored = sem("x_stored")
        x_final = sem("x_final")
        full = [sem(f"full{i}") for i in range(4)]
        free = [sem(f"free{i}") for i in range(4)]
        own_stats = sem("own_stats")
        own_main = sem("own_main")
        own_first = sem("own_first")
        own_tail = sem("own_tail")
        elu_part = sem("elu_part")
        passed = sem("passed")
        relu_neg = sem("relu_neg")
        mneg_ready = sem("mneg_ready")
        ln_var = sem("ln_var")
        ln_rstd = sem("ln_rstd")
        ln_coef = sem("ln_coef")
        h_ready = sem("h_ready")
        deg_ok = sem("deg_ok")
        parts_own = sem("parts_own")
        parts_ready = sem("parts_ready")
        parts_out = sem("parts_out")
        k_head = sem("k_head")
        stacked = sem("stacked")
        folded = sem("folded")
        shift_out = sem("shift_out")
        shift_in = [sem(f"shift_in{c}") for c in range(2)]
        half_out = sem("half_out")
        ones_row = sem("ones_row")
        m0_ready = sem("m0_ready")
        pm_ready = sem("pm_ready")
        pm_used = sem("pm_used")
        mixed = sem("mixed")
        drep_ready = sem("drep_ready")
        weights = sem("weights")
        pv_half = sem("pv_half")
        tile_used = sem("tile_used")
        f2_part = sem("f2_part")
        f2_max = sem("f2_max")
        f2_mid = sem("f2_mid")
        tjdj = sem("tjdj")
        amrep_ready = sem("amrep_ready")
        d_ready = sem("d_ready")
        k_ready = sem("k_ready")
        hb_ready = sem("hb_ready")
        elu_ready = sem("elu_ready")
        elu_sum = sem("elu_sum")

        N_W = 20
        OWN_STATS, OWN_FIRST, OWN_MAIN, OWN_TAIL = 4 + T + 4, 6, 29, 2 * T
        block = ctx.enter_context(nc.Block())

        def wait_full(eng, b, *key):
            u, n = uses[key]
            eng.wait_ge(full[u], b * count[u] + n + 1)
            return U[u]

        def wait_free(b, *key):
            u, n = uses[key]
            nc.tensor.wait_ge(free[u], b * count[u] + n + 1)
            return U[u]

        def wait_read(eng, b, *key):
            u, n = uses[key]
            eng.wait_ge(free[u], b * count[u] + n + 2)

        def wait_fold(eng, b, h, step):
            eng.wait_ge(folded, b * FOLDS * H + fold_order.index((h, step)) + 1)

        def apart(eng):
            eng.sem_inc(passed, 1)

        def freed(ins, *key):
            return ins.then_inc(free[uses[key][0]], 1)

        def filled(ins, *key):
            return ins.then_inc(full[uses[key][0]], 1)

        adj_v = adj.rearrange("b (t p) m -> b t p m", p=P)
        x_v = x_in.rearrange("b (t p) d -> b p t d", p=P)
        out_v = out.rearrange("b (t p) d -> b p t d", p=P)

        def row(ap):
            return ap.partition_broadcast(P)

        def graphs(eng, prologue, main, between, epilogue):
            prologue()
            with eng.Fori(0, NB - 1) as b:
                main(b, True)
                between(b)
            main(NB - 1, False)
            epilogue(NB - 1)

        BETWEEN = [("agg 0", 0), ("tail", 0), ("agg 0", 1), ("tail", 1), ("agg 0", 2), ("agg 0", 3), ("tail", 2),
                   ("agg 0", 4), ("agg 0", 5), ("tail", 3), ("agg 0", 6), ("agg 0", 7), ("agg out", 0), ("tail", 4),
                   ("hidden", 0), ("mlp", 0), ("norm", 1), ("tail", 5), ("tail", 6), ("agg 1", 0), ("agg 1", 1),
                   ("agg 1", 2), ("agg 1", 3), ("tail", 7), ("agg 1", 4), ("agg 1", 5), ("agg 1", 6), ("agg 1", 7),
                   ("agg out", 1)]

        def between_with(tail, start):
            def run(b):
                for what, i in BETWEEN:
                    if what == "tail":
                        tail(b, i)
                    elif what in start:
                        start[what](b + 1, i)
            return run

        def first(start):
            for what, i in BETWEEN:
                if what in start:
                    start[what](0, i)

        @block.sync
        def _(sp):
            n = 0

            def load(dst, src):
                nonlocal n
                n += 1
                sp.dma_start(dst, src).then_inc(w_in, 16)

            def load_adj(b):
                for t in range(T):
                    sp.dma_start(adjN[:, t, :], adj_v[bass.ds(b, 1), t].rearrange("a p m -> (a p) m")).then_inc(adj_in[t], 16)

            def load_x(b):
                sp.dma_start(xin[:, :, :], x_v[bass.ds(b, 1)].rearrange("a p t d -> (a p) t d")).then_inc(x_loaded, 16)

            load_x(0)
            load(w1[:, :], W1)
            load(w2[:, :, :], W2.rearrange("(c p) n -> p c n", p=P))
            for c in range(C1):
                load(b1c[:, c:c + 1], b1[c * P:(c + 1) * P].unsqueeze(1))
            load(b2r[:, :], row(b2))
            load(bgr[:, :], row(bg))
            for i, w in enumerate((Wg, Wq, Wk, Wv, Wo)):
                load(wnat[:, i, :], w)
            load(w3[:, :, :], W3.rearrange("h f o -> f h o"))
            load(b3r[:, :, :].rearrange("p h o -> p (h o)"), row(bias3.rearrange("h o -> (h o)")))
            load(w3v[:, 0, :, :].rearrange("p h o -> p (h o)"), row(w31.rearrange("h o -> (h o)")))
            load(w3v[:, 1, :, :].rearrange("p h o -> p (h o)"), row(w32.rearrange("h o -> (h o)")))
            load(epsc, row(eps0))
            load(wec, row(We.rearrange("h o -> (h o)")))
            load(b31c, row(b31))
            load(b32c, row(b32))
            load(alc, row(alpha))
            assert n == N_W
            load_adj(0)

            def main(b, more):
                for s in range(2):
                    sp.wait_ge(parts_ready, b * 2 + s + 1)
                    sp.dma_start(scratch[s].rearrange("k r n -> r k n"), parts[:, s, :, :]).then_inc(parts_out, 16)
                sp.wait_ge(parts_out, b * 32 + 32)
                for s, dst in ((0, qs), (1, ks)):
                    src = scratch[s].rearrange("k (h d) n -> k d h n", h=H)
                    order = (0, 0, 0, 1, 1, 2) if s == 0 else (0, 1, 2, 0, 1, 0)
                    for i, k in enumerate(order):
                        sp.dma_start(dst[i * HD:(i + 1) * HD, :, :], src[k]).then_inc(stacked, 16)
                for c in range(2):
                    wait_read(sp, b, "maxT", c)
                    sp.dma_start(shifts[c * 4 * N:(c + 1) * 4 * N].rearrange("(k p) -> k p", p=P), mrow[:, c, :]).then_inc(shift_out, 16)
                    sp.wait_ge(shift_out, b * 32 + 16 * c + 16)
                    sp.dma_start(qs[KS:KS + 1, 4 * c:4 * c + 4, :].rearrange("a h n -> a (h n)"),
                                 shifts[c * 4 * N:(c + 1) * 4 * N].unsqueeze(0)).then_inc(shift_in[c], 16)
                if more:
                    for t in MAX_ORDER[-4:]:
                        wait_read(sp, b, "max", H - 1, t)
                        apart(sp)
                    load_adj(b + 1)
                    sp.wait_ge(x_taken, b + 1)
                    apart(sp)
                    load_x(b + 1)

            def store(b):
                sp.wait_ge(x_final, b * T + T)
                apart(sp)
                sp.dma_start(out_v[bass.ds(b, 1)].rearrange("a p t d -> (a p) t d"), hb[:, :, 0:P]).then_inc(x_stored, 16)

            graphs(sp, lambda: None, main, store, store)
            sp.wait_ge(x_stored, NB * 16)

        @block.gpsimd
        def _(pool):
            nc.gpsimd.memset(ident[:, :], 0.0).then_inc(setup_pool, 1)
            nc.gpsimd.memset(one, 1.0).then_inc(setup_pool, 1)
            nc.gpsimd.memset(mhalf, -0.5).then_inc(setup_pool, 1)
            pool.wait_ge(setup_pool, 3)
            nc.gpsimd.affine_select(out=ident[:, :], in_=ident[:, :], compare_op=ALU.not_equal, fill=1.0,
                                    base=0, pattern=[[-1, P]], channel_multiplier=1).then_inc(setup_pool, 1)
            pool.wait_ge(setup_pool, 4)
            pool.wait_ge(w_in, 16 * N_W)

            def norm(b, k):
                for half in range(2):
                    c = slice(half * HT, half * HT + HT)
                    pool.wait_ge(ln_var, b * 8 + 2 * k + half + 1)
                    nc.gpsimd.tensor_tensor(rstd[:, c], ve[:, c], mhalf[:, c], ALU.pow).then_inc(ln_rstd, 1)

            def stats(b):
                norm(b, 0)
                pool.wait_ge(deg_ok, b * 2 + 1)
                nc.gpsimd.tensor_tensor(dpos, degc, mhalf, ALU.pow).then_inc(deg_ok, 1)

                pool.wait_ge(h_ready, b * 4 * T + T)
                nc.gpsimd.tensor_tensor(xin[:, :, :], xin[:, :, :], b2r[:, :].unsqueeze(1).to_broadcast([P, T, P]), ALU.add).then_inc(x_based, 1)

            def main(b, more):
                norm(b, 2)
                for s, (name, src) in enumerate((("q", tmpT), ("k", m0))):
                    wait_read(pool, b, name)
                    nc.gpsimd.tensor_tensor(src[:, :], src[:, :], parts[:, s, 0, :], ALU.subtract).then_inc(parts_own, 1)
                    pool.wait_ge(parts_own, b * 4 + 2 * s + 1)
                    apart(pool)
                    nc.gpsimd.tensor_copy(parts[:, s, 1, :], src[:, :]).then_inc(parts_own, 1)
                    pool.wait_ge(parts_own, b * 4 + 2 * s + 2)
                    nc.gpsimd.tensor_tensor(parts[:, s, 2, :], src[:, :], parts[:, s, 1, :], ALU.subtract).then_inc(parts_ready, 1)
                pool.wait_ge(parts_ready, b * 2 + 2)
                apart(pool)
                nc.gpsimd.memset(ks[KS:KS + 1, :, :], 1.0).then_inc(ones_row, 1)
                pool.wait_ge(ones_row, b + 1)
                for j in range(T):
                    if j:
                        pool.wait_ge(pm_ready, b * T + j)
                    else:
                        pool.wait_ge(parts_ready, b * 2 + 2)
                    apart(pool)
                    nc.gpsimd.tensor_scalar(m0[:, :], adjT[:, j, :], 0.0, MASKED, ALU.is_equal, ALU.mult).then_inc(m0_ready, 1)
                    pool.wait_ge(m0_ready, b * T + j + 1)
                    if j >= 2:
                        pool.wait_ge(pm_used, b * T + j - 1)
                    s = (j % 2) * 2 * N
                    nc.gpsimd.tensor_tensor(pm[:, s:s + N], m0[:, :], adjT[:, j, :], ALU.add)
                    nc.gpsimd.tensor_tensor(pm[:, s + N:s + 2 * N], m0[:, :], adjT[:, j, :], ALU.subtract).then_inc(pm_ready, 1)
                norm(b, 3)
                pool.wait_ge(f2_part, b + 1)
                apart(pool)
                nc.gpsimd.partition_all_reduce(f2x, f2p, P, bass.bass_isa.ReduceOp.max).then_inc(f2_max, 1)
                pool.wait_ge(h_ready, b * 4 * T + 4 * T)
                pool.wait_ge(pm_used, b * T + T)
                for t in range(T):
                    nc.gpsimd.tensor_tensor(hb[:, t, :].rearrange("p (h d) -> p h d", h=H3), b3r[:, :, :],
                                            hN[:, t, :].unsqueeze(1).to_broadcast([P, H3, P]), ALU.add).then_inc(hb_ready, 1)
                wait_full(pool, b, "f1", H3 - 1)
                apart(pool)
                nc.gpsimd.tensor_copy(xs[:, :, :], x[:, :, :]).then_inc(x_kept, 1)
                if more:
                    stats(b + 1)

            def elu_sums(b, t):
                o = 2 * (t % 3)
                pool.wait_ge(elu_ready, b * T + t + 1)
                nc.gpsimd.tensor_tensor(tail[:, o, :], tail[:, o, :], tail[:, o + 1, :], ALU.add).then_inc(elu_part, 1)
                pool.wait_ge(elu_part, b * 2 * T + 2 * t + 1)
                nc.gpsimd.tensor_tensor(tail[:, o, 0:2 * P], tail[:, o, 0:2 * P], tail[:, o, 2 * P:4 * P], ALU.add).then_inc(elu_part, 1)
                pool.wait_ge(elu_part, b * 2 * T + 2 * t + 2)
                nc.gpsimd.tensor_tensor(tail[:, o, 0:P], tail[:, o, 0:P], tail[:, o, P:2 * P], ALU.add).then_inc(elu_sum, 1)

            start = {"norm": norm}
            both = between_with(elu_sums, start)

            def between(b):
                both(b)
                pool.wait_ge(x_stored, b * 16 + 16)

            def prologue():
                stats(0)
                first(start)

            graphs(pool, prologue, main, between, lambda b: [elu_sums(b, t) for t in range(T)])

        @block.scalar
        def _(act):
            act.wait_ge(w_in, 16 * N_W)
            act.wait_ge(setup_pe, 1)
            nc.scalar.activation(wT[:, :, :].rearrange("p k o -> p (k o)"), U[0][:, 0:5 * P], ACT.Copy).then_inc(setup_pe, 1)

            def normalise(b, k, src):
                for t in range(T):
                    if t % HT == 0:
                        act.wait_ge(ln_coef, b * 8 + 2 * k + t // HT + 1)
                    nc.scalar.activation(hN[:, t, :], src[:, t, :], ACT.Relu, bias=nm[:, t:t + 1],
                                         scale=rstd[:, t:t + 1]).then_inc(h_ready, 1)

            def sums(b, t):
                act.wait_ge(adj_max, b * T + t + 1)
                nc.scalar.activation(tmpT[:, :], adjN[:, t, :], ACT.Copy, accum_out=asum[:, t:t + 1]).then_inc(plain_sum, 1)
                act.wait_ge(plain_sum, b * T + t + 1)
                nc.scalar.activation(tmpT[:, :], adjN[:, t, :], ACT.Exp, bias=namax[:, t:t + 1],
                                     accum_out=esum[:, t:t + 1]).then_inc(adj_sum, 1)
                act.wait_ge(adj_sum, b * T + t + 1)

            def adj_turned(b, m, before=None):
                if before is not None:
                    act.wait_ge(mixed, before * T * H3 + (H3 - 1) * T + m + 1)
                to_sbuf(b, adjT[:, m, :], "adjT", m)

            def to_sbuf(b, dst, *key):
                u = wait_full(act, b, *key)
                freed(nc.scalar.activation(dst, u[:, :], ACT.Copy), *key)

            def to_sbuf_halves(b, dst, *key):
                u = wait_full(act, b, *key)
                nc.scalar.activation(dst[:, 0:HALF], u[:, 0:HALF], ACT.Copy).then_inc(half_out, 1)
                freed(nc.scalar.activation(dst[:, HALF:N], u[:, HALF:N], ACT.Copy), *key)

            def hidden(b):
                for c in range(C1):
                    u = wait_full(act, b, "hid", c)
                    freed(nc.scalar.activation(hid[:, c, :], u[:, :], ACT.Relu, bias=b1c[:, c:c + 1]), "hid", c)

            def exp_rho(b, h):
                u = wait_full(act, b, "f1", h)
                if h >= 2:
                    act.wait_ge(mixed, b * T * H3 + (h - 1) * T)
                freed(nc.scalar.activation(rho[:, h % 2, :], u[:, :], ACT.Exp, bias=cb[:, h:h + 1],
                                           scale=-(1.0 - LEAK)), "f1", h)

            def shift_row(b, c):
                u = wait_full(act, b, "maxT", c)
                freed(nc.scalar.activation(mrow[:, c, :], u[0:4 * T, 0:P], ACT.Copy), "maxT", c)

            def main(b, more):
                normalise(b, 2, x)
                to_sbuf_halves(b, hT, "hT", 2)
                u = wait_full(act, b, "q")
                nc.scalar.activation(parts[:, 0, 0, :], u[:, :], ACT.Copy, scale=SCALE)
                freed(nc.scalar.activation(tmpT[:, :], u[:, :], ACT.Copy, scale=SCALE), "q")
                u = wait_full(act, b, "v")
                nc.scalar.activation(va[:, :, :, HD:32], one.unsqueeze(1).unsqueeze(1).to_broadcast([P, T, H, 32 - HD]), ACT.Copy)
                freed(nc.scalar.activation(va[:, :, :, 0:HD], u[:, :].rearrange("p (t h d) -> p t h d", t=T, h=H), ACT.Copy), "v")
                for h in range(H):
                    if h >= 2:
                        wait_fold(act, b, h - 2, FOLDS - 1)
                    for t in MAX_ORDER:
                        if t >= DIRECT:
                            to_sbuf(b, folds[:, h % 2, t - DIRECT, :], "max", h, t)
                    if h == 5:
                        shift_row(b, 0)
                shift_row(b, 1)
                for n in range(T * H):
                    wait_read(act, b, "score", n // H, n % H)
                    nc.scalar.activation(ring[:, n % RING, :], ring[:, n % RING, :], ACT.Exp).then_inc(weights, 1)
                for k in range(NH):
                    for g, dst in ((0, tmpT), (1, hT)):
                        u = wait_full(act, b, "pv", g)
                        c = slice(k * HALF, (k + 1) * HALF)
                        ins = nc.scalar.activation(dst[:, c], u[:, c], ACT.Copy)
                        if k == 0:
                            ins.then_inc(pv_half, 1)
                        else:
                            freed(ins, "pv", g)
                for k in range(NH):
                    u = wait_full(act, b, "oT", k)
                    freed(nc.scalar.activation(hT[:, k * HALF:(k + 1) * HALF], u[:, 0:HALF], ACT.Copy), "oT", k)
                normalise(b, 3, x)
                to_sbuf_halves(b, hT, "hT", 3)
                act.wait_ge(f2_mid, b + 1)
                nc.scalar.activation(tj[:, :, :], f2m[:, :, :], ACT.Exp, scale=1.0 - LEAK)
                nc.scalar.activation(dj[:, :, :], f2m[:, :, :], ACT.Exp, scale=LEAK).then_inc(tjdj, 1)
                exp_rho(b, 0)
                exp_rho(b, 1)
                for j in range(T):
                    if j == T - 1:
                        wait_read(act, b, "amax")
                    else:
                        act.wait_ge(d_ready, b * (T - 1) + j + 1)
                    n = T * H + j
                    act.wait_ge(tile_used, b * TILES + n - RING + 1)
                    nc.scalar.activation(ring[:, n % RING, :], adjT[:, j, :], ACT.Exp).then_inc(weights, 1)
                    act.wait_ge(weights, b * (T * H + T) + n + 1)
                    nc.scalar.activation(adjT[:, j, :], adjT[:, j, :], ACT.Exp, scale=PENALTY).then_inc(k_ready, 1)
                to_sbuf(b, caT[:, :], "ca")
                for h in range(H3):
                    if more and h == 3:
                        for m in range(T - 2):
                            adj_turned(b + 1, m, b)
                    to_sbuf(b, numT[:, h, :], "num", h)
                    if more and h == 3:
                        adj_turned(b + 1, T - 2, b)
                    u = wait_full(act, b, "den", h)
                    freed(nc.scalar.activation(denS[:, h, :], u[:, 0:HALF], ACT.Copy), "den", h)
                    if h + 2 < H3:
                        exp_rho(b, h + 2)
                    if more and h < 2:
                        for t in range(h * HT, h * HT + HT):
                            sums(b + 1, t)
                    if more and h == 2:
                        normalise(b + 1, 0, xin)
                    if more and h == 3:
                        adj_turned(b + 1, T - 1, b)

            def elus(b, t):
                o = 2 * (t % 3)
                wait_read(act, b, "tail", t)
                nc.scalar.activation(tail[:, o + 1, :], tail[:, o, :], ACT.Relu, scale=-1.0).then_inc(relu_neg, 1)
                act.wait_ge(relu_neg, b * T + t + 1)
                nc.scalar.activation(tail[:, o + 1, :], tail[:, o + 1, :], ACT.Exp, scale=-1.0)
                nc.scalar.activation(tail[:, o, :], tail[:, o, :], ACT.Relu).then_inc(elu_ready, 1)

            start = {"agg out": lambda b, i: to_sbuf_halves(b, tmpT, "agg", i),
                     "hidden": lambda b, i: hidden(b),
                     "norm": lambda b, i: normalise(b, 1, x)}

            def prologue():
                normalise(0, 0, xin)
                for t in range(T):
                    adj_turned(0, t)
                for t in range(T):
                    sums(0, t)
                first(start)

            graphs(act, prologue, main, between_with(elus, start), lambda b: [elus(b, t) for t in range(T)])

        @block.tensor
        def _(pe):
            for i in range(4):
                pe.sem_inc(free[i], 1)
            pe.wait_ge(setup_pool, 4)
            pe.wait_ge(w_in, 16 * N_W)
            for i in range(5):
                last = pe.transpose(U[0][:, i * P:(i + 1) * P], wnat[:, i, :], ident[:, :])
            last.then_inc(setup_pe, 1)
            pe.wait_ge(setup_pe, 2)
            pe.wait_ge(setup_dve, 3)
            w3_all = w3[:, :, :].rearrange("p h o -> p (h o)")

            def half(ap, i):
                return ap[:, i * HALF:(i + 1) * HALF]

            def halves(u, lhsT, rhs, second=None):
                for i in range(NH):
                    if i and second:
                        second()
                    last = pe.matmul(half(u, i), lhsT, half(rhs, i), start=True, stop=True)
                return last

            def aggregate(b, i, m, diag):
                u = wait_free(b, "agg", i) if m == 0 else U[uses["agg", i][0]]
                pe.wait_ge(h_ready, b * 4 * T + i * T + m + 1)
                for k in range(NH):
                    pe.matmul(half(u, k), hN[:, m, :], half(adjT[:, m, :], k), start=(m == 0), stop=False, skip_group_check=True)
                last = pe.matmul(u[:, m * P:(m + 1) * P], hN[:, m, :], diag, start=False, stop=(m == T - 1), skip_group_check=True)
                if m == T - 1:
                    filled(last, "agg", i)

            def node_rows(b, lhs, weights_T, *key, second=None):
                for k in range(2):
                    u = wait_free(b, *key, k)
                    if k and second:
                        second()
                    for t in range(HT):
                        n = k * HT + t
                        last = pe.matmul(u[:, t * P:(t + 1) * P], lhs[:, n * P:(n + 1) * P], weights_T, start=True, stop=True)
                    filled(last, *key, k)

            def features_up(b, k, *key):
                u = wait_free(b, *key)
                for t in range(T):
                    pe.wait_ge(h_ready, b * 4 * T + k * T + t + 1)
                    last = pe.transpose(u[:, t * P:(t + 1) * P], hN[:, t, :], ident[:, :])
                filled(last, *key)

            def made(b, *key):
                wait_read(pe, b, *key)

            def half_made(b, i):
                pe.wait_ge(half_out, b * 4 + i + 1)

            def turn_adj(b, m):
                u = wait_free(b, "adjT", m)
                for t in range(T):
                    if m == 0:
                        pe.wait_ge(adj_in[t], b * 16 + 16)
                    last = pe.transpose(u[:, t * P:(t + 1) * P], adjN[:, t, m * P:(m + 1) * P], ident[:, :])
                filled(last, "adjT", m)

            def hidden(b):
                half_made(b, 0)
                for c in range(C1):
                    u = wait_free(b, "hid", c)
                    filled(halves(u, w1[:, c * P:(c + 1) * P], tmpT, None if c else lambda: made(b, "agg", 0)), "hid", c)

            def mlp_out(b):
                for c in range(C1):
                    made(b, "hid", c)
                for k in range(2):
                    u = wait_free(b, "mlp", k)
                    for t in range(HT):
                        n = k * HT + t
                        for c in range(C1):
                            last = pe.matmul(u[:, t * P:(t + 1) * P], hid[:, c, n * P:(n + 1) * P], w2[:, c, :], start=(c == 0), stop=(c == C1 - 1))
                    filled(last, "mlp", k)

            def attend(b, j, g, k):
                pv = U[uses["pv", g][0]]
                if k == 0:
                    pe.wait_ge(weights, b * (T * H + T) + j * H + 4 * g + 4)
                for h4 in range(4):
                    h = 4 * g + h4
                    last = pe.matmul(pv[32 * h4:32 * h4 + 32, k * HALF:(k + 1) * HALF], va[:, j, h, :],
                                     half(ring[:, (j * H + h) % RING, :], k),
                                     start=(j == 0), stop=(j == T - 1), tile_position=(0, 32 * h4), skip_group_check=True)
                if k == 1:
                    last.then_inc(tile_used, 4)

            def sum_columns(b, h, j):
                d = wait_free(b, "den", h) if j == 1 else U[uses["den", h][0]]
                n = T * H + T + h * T + j
                for par in range(2):
                    for k in range(NH):
                        c = 32 * (par * NH + k)
                        last = pe.matmul(d[c:c + 32, 0:HALF], drep[:, j - 1 + par, h, :], half(ring[:, (n - 1 + par) % RING, :], k),
                                         start=(j == 1), stop=(j == T - 1), tile_position=(0, c), skip_group_check=True)
                last.then_inc(tile_used, 2)

            def turn_sums(b, h):
                u = wait_free(b, "denT", h)
                made(b, "den", h)
                for c in range(HALF // P):
                    last = pe.matmul(u[:, c * 4:c * 4 + 4], denS[:, h, c * P:(c + 1) * P], ident[:, 0:P:32], start=True, stop=True)
                filled(last, "denT", h)

            def f1_rows(b, h):
                u = wait_free(b, "f1", h)
                filled(halves(u, u12[:, 0, h:h + 1].to_broadcast([P, P]), hT), "f1", h)

            def main(b, more):
                half_made(b, 1)
                node_rows(b, tmpT, wT[:, 0, :], "lin1", second=lambda: made(b, "agg", 1))
                features_up(b, 2, "hT", 2)
                half_made(b, 2)
                u = wait_free(b, "q")
                filled(halves(u, wT[:, 1, :], hT, lambda: made(b, "hT", 2)), "q")
                u = wait_free(b, "k")
                filled(halves(u, wT[:, 2, :], hT), "k")
                u = wait_free(b, "v")
                for t in range(T):
                    last = pe.matmul(u[:, t * P:(t + 1) * P], hT[:, t * P:(t + 1) * P], wT[:, 3, :], start=True, stop=True)
                filled(last, "v")
                made(b, "q")
                for h in range(H):
                    pe.wait_ge(k_head, b * H + h + 1)
                    for t in MAX_ORDER:
                        u = wait_free(b, "max", h, t)
                        for i in range(NH):
                            last = pe.matmul(half(u, i), parts[:, 0, 0, t * P:(t + 1) * P], half(kh[h], i), start=True, stop=t < DIRECT)
                        if t >= DIRECT:
                            if h == 0:
                                pe.wait_ge(mask_ready, b * T + t + 1)
                            for i in range(NH):
                                last = pe.matmul(half(u, i), identB[:, :], half(maskN[t], i), start=False, stop=True)
                        filled(last, "max", h, t)
                    if h == 5:
                        turn_shifts(b, 0)
                pe.wait_ge(stacked, b * 192 + 192)
                pe.wait_ge(ones_row, b + 1)
                made(b, "v")
                wait_free(b, "pv", 0)
                for j in range(T):
                    for g in range(2):
                        if j == 0:
                            pe.wait_ge(shift_in[g], b * 16 + 16)
                        before = (j, 0) if g else (j - 1, 1)
                        for h4 in range(4):
                            h = 4 * g + h4
                            u = wait_free(b, "score", j, h)
                            filled(halves(u, ks[0:KS + 1, h, j * P:(j + 1) * P], qs[0:KS + 1, h, :]), "score", j, h)
                            if (j, h) == (0, 1):
                                turn_shifts(b, 1)
                                wait_free(b, "pv", 1)
                            if before[0] >= 0 and h4 >= 2:
                                attend(b, *before, h4 - 2)
                attend(b, T - 1, 1, 0)
                attend(b, T - 1, 1, 1)
                pe.wait_ge(tile_used, b * TILES + T * H)
                pe.sem_inc(full[uses["pv", 0][0]], 1)
                pe.sem_inc(full[uses["pv", 1][0]], 1)
                for k in range(NH):
                    u = wait_free(b, "oN", k)
                    for g, src in ((0, tmpT), (1, hT)):
                        if k == 0:
                            pe.wait_ge(pv_half, b * 2 + g + 1)
                        else:
                            made(b, "pv", g)
                        for t in range(HT):
                            n = k * HT + t
                            last = pe.transpose(u[:, g * HALF + t * P:g * HALF + (t + 1) * P], src[:, n * P:(n + 1) * P], ident[:, :])
                    filled(last, "oN", k)
                for k in range(NH):
                    u = wait_free(b, "oT", k)
                    made(b, "oN", k)
                    for t in range(HT):
                        last = pe.transpose(u[:, t * P:(t + 1) * P], hN[:, k * HT + t, :], ident[:, :])
                    filled(last, "oT", k)
                for k in range(NH):
                    u = wait_free(b, "wo", k)
                    made(b, "oT", k)
                    for t in range(HT):
                        n = k * HT + t
                        last = pe.matmul(u[:, t * P:(t + 1) * P], hT[:, n * P:(n + 1) * P], wT[:, 4, :], start=True, stop=True)
                    filled(last, "wo", k)
                u = wait_free(b, "amax")
                pe.wait_ge(amrep_ready, b + 1)
                for t in range(T):
                    last = pe.transpose(u[:, t * P:(t + 1) * P], m0[:, t * P:(t + 1) * P], ident[:, :])
                filled(last, "amax")
                features_up(b, 3, "hT", 3)
                half_made(b, 3)
                u = wait_free(b, "f2")
                for t in range(T):
                    if t == HT:
                        made(b, "hT", 3)
                    last = pe.matmul(u[:, t * H3:(t + 1) * H3], hT[:, t * P:(t + 1) * P], u12[:, 1, :], start=True, stop=True)
                filled(last, "f2")
                f1_rows(b, 0)
                f1_rows(b, 1)

                def softmax_adj(j):
                    u = wait_free(b, "ca") if j == 0 else U[uses[("ca",)][0]]
                    n = T * H + j
                    pe.wait_ge(weights, b * (T * H + T) + n + 1)
                    for k in range(NH):
                        last = pe.matmul(half(u, k), hN[:, j, :], half(ring[:, n % RING, :], k), start=(j == 0), stop=(j == T - 1),
                                         skip_group_check=True)
                    last.then_inc(tile_used, 1)

                for t in range(T):
                    u = wait_free(b, "fts", t)
                    filled(pe.matmul(u[:, 0:H3 * P], hT[:, t * P:(t + 1) * P], w3_all, start=True, stop=True), "fts", t)
                    if t:
                        softmax_adj(t - 1)
                softmax_adj(T - 1)
                pe.wait_ge(tile_used, b * TILES + T * H + T)
                pe.sem_inc(full[uses[("ca",)][0]], 1)
                pe.wait_ge(drep_ready, b + 1)
                made(b, "fts", T - 2)
                made(b, "fts", T - 1)
                for h in range(H3):
                    u = wait_free(b, "num", h)
                    for j in range(T):
                        pe.wait_ge(mixed, b * T * H3 + h * T + j + 1)
                        for k in range(NH):
                            last = pe.matmul(half(u, k), vals[:, j, h, :], half(ring[:, (T * H + T + h * T + j) % RING, :], k),
                                             start=(j == 0), stop=(j == T - 1), skip_group_check=True)
                        if j == T - 1:
                            filled(last, "num", h)
                        if j % 2:
                            sum_columns(b, h, j)
                        if j == 2 and h:
                            turn_sums(b, h - 1)
                        if j == 5 and h + 2 < H3:
                            f1_rows(b, h + 2)
                        if more and h == H3 - 1 and j:
                            turn_adj(b + 1, j - 1)
                    pe.wait_ge(tile_used, b * TILES + T * H + T + (h + 1) * T)
                    pe.sem_inc(full[uses["den", h][0]], 1)
                turn_sums(b, H3 - 1)
                if more:
                    turn_adj(b + 1, T - 1)

            def turn_shifts(b, c):
                u = wait_free(b, "maxT", c)
                pe.wait_ge(mneg_ready, b * 2 + c + 1)
                apart(pe)
                filled(pe.transpose(u[0:4 * T, 0:P], mneg[:, 4 * c:4 * c + 4, :].rearrange("p h t -> p (h t)"), ident[:, :]), "maxT", c)

            def finish_rows(b, t):
                u = wait_free(b, "tail", t)
                if t == 0:
                    made(b, "ca")
                    for h in range(H3):
                        made(b, "num", h)
                for h in range(H3):
                    pe.transpose(u[:, h * P:(h + 1) * P], numT[:, h, t * P:(t + 1) * P], ident[:, :])
                filled(pe.matmul(u[:, HALF:2 * HALF], caT[:, t * P:(t + 1) * P], w3_all, start=True, stop=True), "tail", t)

            start = {"agg 0": lambda b, m: aggregate(b, 0, m, identE[:, :]),
                     "hidden": lambda b, i: hidden(b),
                     "mlp": lambda b, i: mlp_out(b),
                     "agg 1": lambda b, m: aggregate(b, 1, m, ident[:, :])}

            def prologue():
                for t in range(T):
                    turn_adj(0, t)
                first(start)

            graphs(pe, prologue, main, between_with(finish_rows, start), lambda b: [finish_rows(b, t) for t in range(T)])

        @block.vector
        def _(dve):
            V = nc.vector
            k = [0]

            def setup(ins):
                k[0] += 1
                ins.then_inc(own_main, 1)
                dve.wait_ge(own_main, k[0])

            dve.wait_ge(w_in, 16 * N_W)
            dve.wait_ge(setup_pool, 4)
            setup(V.tensor_scalar(oneE, epsc, 1.0, None, ALU.add))
            setup(V.tensor_copy(identB[:, :], ident[:, :]))
            setup(V.tensor_reduce(headm[:, :], ident[:, :].rearrange("p (h d) -> p h d", h=H), AX.X, ALU.add))
            setup(V.tensor_scalar(identE[:, :], ident[:, :], oneE, None, ALU.mult))
            setup(V.tensor_scalar(wneg, wec, -1.0, None, ALU.mult))
            setup(V.tensor_tensor(wabs, wec, wneg, ALU.max))
            setup(V.tensor_scalar(wabs, wabs, TINY, None, ALU.max))
            setup(V.tensor_scalar(wpos, wec, 0.0, None, ALU.max))
            setup(V.tensor_scalar(signf[:, :], wec, 0.0, float(N), ALU.is_lt, ALU.mult))
            setup(V.tensor_copy(signi[:, :], signf[:, :]))
            setup(V.tensor_scalar(oma, alc, -1.0, 1.0, ALU.mult, ALU.add))
            for i in range(2):
                setup(V.tensor_tensor(utmp[:, :, :], w3[:, :, :], w3v[:, i, :, :], ALU.mult))
                setup(V.tensor_reduce(u12[:, i, :], utmp[:, :, :], AX.X, ALU.add))
            dve.sem_inc(setup_dve, 3)
            SET = k[0]
            sign = [dve.value_load(signi[0:1, h:h + 1], min_val=0, max_val=N) for h in range(H)]

            chains = {"stats": (own_stats, OWN_STATS, 0),
                      "first": (own_first, OWN_FIRST, 0), "main": (own_main, OWN_MAIN, SET), "tail": (own_tail, OWN_TAIL, 0)}
            steps = {}

            def begin(b, phase):
                steps[phase] = [b, 0]

            def own(phase, ins):
                s, per_graph, base = chains[phase]
                steps[phase][1] += 1
                b, c = steps[phase]
                ins.then_inc(s, 1)
                s_at = b * per_graph + base + c
                dve.wait_ge(s, s_at)

            def end(phase):
                assert steps[phase][1] == chains[phase][1], (phase, steps[phase][1])

            def own_freed(b, ins, *key):
                freed(ins, *key)
                wait_read(dve, b, *key)

            def layer_norm(b, i, src, phase, ready=None, with_degree=False):
                def coefficients(k):
                    c = slice(k * HT, k * HT + HT)
                    dve.wait_ge(ln_rstd, b * 8 + 2 * i + k + 1)
                    if with_degree:
                        own(phase, V.tensor_tensor(rstd[:, c], rstd[:, c], dinv[:, c], ALU.mult))
                    V.scalar_tensor_tensor(nm[:, c], mv[:, c, 0], -1.0, rstd[:, c], ALU.mult, ALU.mult).then_inc(ln_coef, 1)

                for k in range(2):
                    if ready:
                        ready(k)
                    if k:
                        coefficients(k - 1)
                    for t in range(k * HT, k * HT + HT):
                        last = V.bn_stats(st[:, t, :], src[:, t, :])
                    own(phase, last)
                    apart(dve)
                    for t in range(k * HT, k * HT + HT):
                        last = V.bn_aggr(mv[:, t, :], st[:, t, :])
                    own(phase, last)
                    c = slice(k * HT, k * HT + HT)
                    V.tensor_scalar(ve[:, c], mv[:, c, 1], LN_EPS, None, ALU.add).then_inc(ln_var, 1)
                coefficients(1)

            def half_nodes(u):
                return u[:, 0:HALF].rearrange("p (t d) -> p t d", t=HT)

            def adj_max_tile(b, t):
                dve.wait_ge(adj_in[t], b * 16 + 16)
                own("stats", V.tensor_reduce(amax[:, t:t + 1], adjN[:, t, :], AX.X, ALU.max))
                V.tensor_scalar(namax[:, t:t + 1], amax[:, t:t + 1], -1.0, None, ALU.mult).then_inc(adj_max, 1)

            def first_norm(b):
                dve.wait_ge(x_loaded, b * 16 + 16)
                layer_norm(b, 0, xin, "stats")

            def degrees(b):
                dve.wait_ge(adj_sum, b * T + T)
                own("stats", V.tensor_scalar(deg, asum, 1.0, None, ALU.add))
                V.tensor_scalar(degc, deg, 1e-30, None, ALU.max).then_inc(deg_ok, 1)
                dve.wait_ge(deg_ok, b * 2 + 2)
                own("stats", V.tensor_scalar(deg, deg, 0.0, None, ALU.is_gt))
                own("stats", V.tensor_tensor(dinv, deg, dpos, ALU.mult))
                own("stats", V.reciprocal(re, esum))
                end("stats")

            def masks(b):
                wait_full(dve, b, "adjT", T - 1)
                for t in range(T):
                    if t:
                        dve.wait_ge(mask_ready, b * T + t)
                    V.tensor_scalar(maskN[t], adjN[:, t, :], 0.0, MASKED, ALU.is_equal, ALU.mult).then_inc(mask_ready, 1)

            def layer_0(b):
                dve.wait_ge(x_based, b + 1)
                for k in range(2):
                    u = wait_full(dve, b, "mlp", k)
                    c = slice(k * HT, (k + 1) * HT)
                    freed(V.tensor_tensor(x[:, c, :], xin[:, c, :], half_nodes(u), ALU.add), "mlp", k)
                begin(b, "first")
                layer_norm(b, 1, x, "first", ready=lambda k: wait_read(dve, b, "mlp", k), with_degree=True)
                end("first")
                dve.sem_inc(x_taken, 1)

            def main(b, more):
                begin(b, "main")
                def add_lin1(k):
                    c = slice(k * HT, (k + 1) * HT)
                    u = wait_full(dve, b, "lin1", k)
                    for t in range(HT):
                        n = k * HT + t
                        ins = V.scalar_tensor_tensor(hN[:, n, :], u[:, t * P:(t + 1) * P], dinv[:, n:n + 1], bgr[:, :], ALU.mult, ALU.add)
                    own_freed(b, ins, "lin1", k)
                    own("main", V.scalar_tensor_tensor(x[:, c, :], hN[:, c, :], 0.0, x[:, c, :], ALU.max, ALU.add))

                layer_norm(b, 2, x, "main", ready=add_lin1)
                u = wait_full(dve, b, "k")
                V.tensor_copy(parts[:, 1, 0, :], u[:, :])
                own_freed(b, V.tensor_copy(m0[:, :], u[:, :]), "k")
                for h in range(H):
                    V.tensor_scalar(kh[h], parts[:, 1, 0, :], headm[:, h:h + 1], None, ALU.mult).then_inc(k_head, 1)
                def fold(h, step):
                    width = HALF >> max(step - 1, 0)
                    if step < 2:
                        wait_read(dve, b, "max", h, DIRECT + 3 * step + 2)
                        f = folds[:, h % 2, 3 * step:3 * step + 3, :]
                    else:
                        wait_fold(dve, b, h, step - 1)
                        f = folds[:, h % 2, 0:T - DIRECT, :]
                    if step == FOLDS - 1:
                        ins = V.tensor_reduce(mx[:, h, DIRECT:T], f[:, :, 0:2 * width], AX.X, ALU.max)
                    else:
                        ins = V.tensor_tensor(f[:, :, 0:width], f[:, :, 0:width], f[:, :, width:2 * width], ALU.max)
                    ins.then_inc(folded, 1)

                def direct_max(h, t):
                    u = wait_full(dve, b, "max", h, t)
                    apart(dve)
                    freed(V.tensor_tensor_reduce(u[:, :], u[:, :], maskN[t], 1.0, 3.0 * MASKED, ALU.add, ALU.max,
                                                 mx[:, h, t:t + 1]), "max", h, t)

                def shifts_of(c):
                    wait_fold(dve, b, 4 * c + 3, FOLDS - 1)
                    wait_read(dve, b, "max", 4 * c + 3, DIRECT - 1)
                    g = slice(4 * c, 4 * c + 4)
                    own("main", V.tensor_tensor(mneg[:, g, :], wpos[:, g].unsqueeze(2).to_broadcast([P, 4, T]),
                                                amax.unsqueeze(1).to_broadcast([P, 4, T]), ALU.mult))
                    own("main", V.tensor_tensor(mneg[:, g, :], mneg[:, g, :], mx[:, g, :], ALU.add))
                    V.tensor_scalar(mneg[:, g, :], mneg[:, g, :], -1.0, None, ALU.mult).then_inc(mneg_ready, 1)

                for h in range(H):
                    direct_max(h, 0)
                    if h:
                        fold(h - 1, 1)
                        fold(h - 1, 2)
                    direct_max(h, 1)
                    fold(h, 0)
                    if h:
                        fold(h - 1, 3)
                        fold(h - 1, 4)
                        fold(h - 1, 5)
                    if h == 4:
                        shifts_of(0)
                for step in range(1, FOLDS):
                    fold(H - 1, step)
                shifts_of(1)

                for j in range(T):
                    dve.wait_ge(pm_ready, b * T + j + 1)
                    for h in range(H):
                        n = j * H + h
                        u = wait_full(dve, b, "score", j, h)
                        if n >= RING:
                            dve.wait_ge(tile_used, b * TILES + n - RING + 1)
                        ins = V.scalar_tensor_tensor(ring[:, n % RING, :], pm[:, bass.ds(sign[h] + (j % 2) * 2 * N, N)],
                                                     wabs[:, h:h + 1], u[:, :], ALU.mult, ALU.add)
                        freed(ins, "score", j, h)
                    wait_read(dve, b, "score", j, H - 2)
                    wait_read(dve, b, "score", j, H - 1)
                    dve.sem_inc(pm_used, 1)
                for k in range(NH):
                    u = wait_full(dve, b, "oN", k)
                    o4 = u[:, :].rearrange("p (g t h d) -> p g t h d", g=2, t=HT, h=4)
                    own("main", V.reciprocal(rden[:, :, :, :], o4[:, :, :, :, HD]))
                    for g in range(2):
                        ins = V.tensor_tensor(hN[:, k * HT:(k + 1) * HT, g * 4 * HD:(g + 1) * 4 * HD].rearrange("p t (h d) -> p t h d", h=4),
                                              o4[:, g, :, :, 0:HD], rden[:, g, :, :].unsqueeze(3).to_broadcast([P, HT, 4, HD]), ALU.mult)
                    own_freed(b, ins, "oN", k)
                dve.wait_ge(pm_ready, b * T + T)
                V.tensor_copy(m0[:, :].rearrange("p (t d) -> p t d", t=T), amax.unsqueeze(2).to_broadcast([P, T, P])).then_inc(amrep_ready, 1)
                own("main", V.tensor_tensor(r2[:, :, :], oma.unsqueeze(2).to_broadcast([P, H3, T]), re.unsqueeze(1).to_broadcast([P, H3, T]), ALU.mult))

                def add_wo(k):
                    u = wait_full(dve, b, "wo", k)
                    c = slice(k * HT, (k + 1) * HT)
                    own_freed(b, V.tensor_tensor(x[:, c, :], x[:, c, :], half_nodes(u), ALU.add), "wo", k)

                layer_norm(b, 3, x, "main", ready=add_wo)
                u = wait_full(dve, b, "f2")
                own_freed(b, V.tensor_tensor(f2[:, :, :], u[:, 0:T * H3].rearrange("p (t h) -> p t h", t=T),
                                             b32c.unsqueeze(1).to_broadcast([P, T, H3]), ALU.add), "f2")
                V.tensor_reduce(f2p, f2[:, :, :].rearrange("p t h -> p h t"), AX.X, ALU.max).then_inc(f2_part, 1)
                dve.wait_ge(f2_max, b + 1)
                own("main", V.tensor_tensor(cb, b31c, f2x, ALU.add))
                own("main", V.tensor_scalar(cb, cb, -(1.0 - LEAK), None, ALU.mult))
                V.tensor_tensor(f2m[:, :, :], f2[:, :, :], f2x.unsqueeze(1).to_broadcast([P, T, H3]), ALU.subtract).then_inc(f2_mid, 1)
                am = wait_full(dve, b, "amax")
                for j in range(T):
                    ins = V.tensor_tensor(adjT[:, j, :], adjT[:, j, :], am[:, :], ALU.subtract)
                    if j < T - 1:
                        ins.then_inc(d_ready, 1)
                    else:
                        freed(ins, "amax")
                    if j == 0:
                        dve.wait_ge(tjdj, b + 1)
                    u = wait_full(dve, b, "fts", j)
                    freed(V.tensor_tensor(vals[:, j, :, :], u[:, 0:H3 * P].rearrange("p (h d) -> p h d", h=H3),
                                          dj[:, j, :].unsqueeze(2).to_broadcast([P, H3, P]), ALU.mult), "fts", j)
                V.tensor_copy(drep[:, :, :, :], dj[:, :, :].unsqueeze(3).to_broadcast([P, T, H3, 32])).then_inc(drep_ready, 1)
                if more:
                    begin(b + 1, "stats")
                for h in range(H3):
                    wait_read(dve, b, "f1", h)
                    own("main", V.tensor_scalar(rho[:, h % 2, :], rho[:, h % 2, :], 1.0, None, ALU.min))
                    for j in range(T):
                        if h == 0:
                            dve.wait_ge(k_ready, b * T + j + 1)
                        n = T * H + T + h * T + j
                        dve.wait_ge(tile_used, b * TILES + n - RING + 1)
                        V.scalar_tensor_tensor(ring[:, n % RING, :], rho[:, h % 2, :], tj[:, j, h:h + 1], adjT[:, j, :],
                                               ALU.max, ALU.mult).then_inc(mixed, 1)
                        if more and h < 2 and j % 2 == 0:
                            adj_max_tile(b + 1, h * HT + j // 2)
                        if more and (h, j) == (2, T // 2):
                            first_norm(b + 1)
                        if more and (h, j) == (3, T // 2):
                            degrees(b + 1)
                    if h:
                        columns(b, h - 1)
                columns(b, H3 - 1)
                own("main", V.reciprocal(r1[:, :, :], den[:, :, :]))
                own("main", V.tensor_tensor(r1[:, :, :], r1[:, :, :], alc.unsqueeze(2).to_broadcast([P, H3, T]), ALU.mult))
                end("main")

            def columns(b, h):
                u = wait_full(dve, b, "denT", h)
                d4 = u[:, 0:16].rearrange("p (c g) -> p c g", g=4)
                for k in range(NH):
                    last = V.tensor_copy(den[:, h, k * 4:k * 4 + 4], d4[:, :, k])
                own("main", last)
                for k in range(NH):
                    last = V.tensor_tensor(den[:, h, k * 4:k * 4 + 4], den[:, h, k * 4:k * 4 + 4], d4[:, :, NH + k], ALU.add)
                own_freed(b, last, "denT", h)

            def combine(b, t):
                o = 2 * (t % 3)
                u = wait_full(dve, b, "tail", t)
                dve.wait_ge(hb_ready, b * T + t + 1)
                if t >= 3:
                    finish(b, t - 3)
                for h in range(H3):
                    ins = V.scalar_tensor_tensor(tail[:, o, h * P:(h + 1) * P], u[:, h * P:(h + 1) * P], r1[:, h, t:t + 1],
                                                 hb[:, t, h * P:(h + 1) * P], ALU.mult, ALU.add)
                own("tail", ins)
                for h in range(H3):
                    ins = V.scalar_tensor_tensor(tail[:, o, h * P:(h + 1) * P], u[:, HALF + h * P:HALF + (h + 1) * P], r2[:, h, t:t + 1],
                                                 tail[:, o, h * P:(h + 1) * P], ALU.mult, ALU.add)
                freed(ins, "tail", t)

            def finish(b, t):
                o = 2 * (t % 3)
                dve.wait_ge(elu_sum, b * T + t + 1)
                own("tail", V.tensor_scalar(tail[:, o, 0:P], tail[:, o, 0:P], 1.0 / H3, -1.0, ALU.mult, ALU.add))
                V.tensor_tensor(hb[:, t, 0:P], xs[:, t, :], tail[:, o, 0:P], ALU.add).then_inc(x_final, 1)
                dve.wait_ge(x_final, b * T + t + 1)

            start = {"norm": lambda b, i: layer_0(b)}
            both = between_with(combine, start)

            def between(b):
                begin(b, "tail")
                masks(b + 1)
                dve.wait_ge(x_kept, b + 1)
                both(b)
                for t in range(T - 3, T):
                    finish(b, t)
                end("tail")

            def prologue():
                begin(0, "stats")
                first_norm(0)
                for t in range(T):
                    adj_max_tile(0, t)
                degrees(0)
                masks(0)
                first(start)

            def epilogue(b):
                begin(b, "tail")
                dve.wait_ge(x_kept, b + 1)
                for t in range(T):
                    combine(b, t)
                for t in range(T - 3, T):
                    finish(b, t)
                end("tail")

            graphs(dve, prologue, main, between, epilogue)


_INS = ['x', 'adj', 'L0_gnn_eps', 'L0_gnn_W1', 'L0_gnn_b1', 'L0_gnn_W2', 'L0_gnn_b2', 'L1_gnn_W', 'L1_gnn_b',
        'L2_gnn_W_q', 'L2_gnn_W_k', 'L2_gnn_W_v', 'L2_gnn_W_e', 'L2_gnn_W_o', 'L3_gnn_W', 'L3_gnn_w1', 'L3_gnn_b1',
        'L3_gnn_w2', 'L3_gnn_b2', 'L3_gnn_alpha', 'L3_gnn_bias']


def kernel(**inputs):
    import numpy as _np
    import concourse.bacc as _bacc
    from concourse import mybir as _mybir
    from concourse.bass_utils import run_bass_kernel_spmd as _run

    nc = _bacc.Bacc("TRN2", target_bir_lowering=False, num_devices=1)
    arrays, args = {}, []
    for name in _INS:
        a = _np.ascontiguousarray(inputs[name])
        arrays[f"in_{name}"] = a
        args.append(nc.dram_tensor(f"in_{name}", a.shape, _mybir.dt.from_np(a.dtype), kind="ExternalInput").ap())
    shape = inputs['x'].shape
    out = nc.dram_tensor("out_x", shape, _mybir.dt.float32, kind="ExternalOutput").ap()
    scratch = nc.dram_tensor("scratch_qk_parts", (2, 3, shape[2], shape[1]), _mybir.dt.bfloat16, kind="Internal").ap()
    shifts = nc.dram_tensor("scratch_shifts", (inputs['L2_gnn_W_e'].shape[0] * shape[1],), _mybir.dt.bfloat16, kind="Internal").ap()
    graph_layers(nc, *args, out, scratch, shifts)
    r = _run(nc, [arrays], core_ids=[0])
    return r.results[0]["out_x"]
```
